# Optimizing a Trainium2 kernel written in Bass

```python
import numpy as np
import jax
import jax.numpy as jnp

def _softmax(x, axis=-1):
    return jax.nn.softmax(x, axis=axis)

def _gelu(x):
    return jax.nn.gelu(x, approximate=True)

def _silu(x):
    return jax.nn.silu(x)

def _sigmoid(x):
    return jax.nn.sigmoid(x)

def _layernorm(x, axis=-1, eps=1e-05):
    m = jnp.mean(x, axis=axis, keepdims=True)
    v = jnp.var(x, axis=axis, keepdims=True)
    return (x - m) / jnp.sqrt(v + eps)

def _scatter_add(tgt, idx, src, axis=0):
    return tgt.at[idx].add(src)

def _segment_sum(src, seg, n):
    return jax.ops.segment_sum(src, seg, n)
kernel_name = 'mk_seq_postln_d1_jaxref_r4_7acbf6'

def setup_inputs(seed: int=0):
    np.random.seed(seed)
    _w = jnp.asarray

    def _L0_attn_setup():
        import jax, jax.numpy as jnp
        import numpy as np
        D_MODEL = 256
        D_STATE = 16
        D_CONV = 4
        EXPAND = 2
        D_INNER = D_MODEL * EXPAND

        def soft_clamp(x, lo, hi, sharp):
            c = (hi + lo) / 2.0
            r = (hi - lo) / 2.0
            return jnp.tanh((x - c) / (r + 1e-08) * sharp) / sharp * r + c
        key = jax.random.key(seed)
        ks = jax.random.split(key, 9)
        B, L = (2, 256)
        x = jax.random.normal(ks[0], (B, L, D_MODEL), jnp.float32)
        norm_w = jnp.ones((D_MODEL,), jnp.float32)
        W_in = jax.random.normal(ks[1], (2 * D_INNER, D_MODEL), jnp.float32) * 0.02
        conv_w = jax.random.normal(ks[2], (D_INNER, 1, D_CONV), jnp.float32) * 0.02
        conv_b = jnp.zeros((D_INNER,), jnp.float32)
        W_dt = jax.random.normal(ks[3], (D_INNER, D_INNER), jnp.float32) * 0.02
        b_dt = jnp.full((D_INNER,), -2.0, jnp.float32)
        W_B = jax.random.normal(ks[4], (D_STATE, D_INNER), jnp.float32) * 0.02
        W_C = jax.random.normal(ks[5], (D_STATE, D_INNER), jnp.float32) * 0.02
        A_log = jax.random.normal(ks[6], (D_INNER, D_STATE), jnp.float32) * 0.1
        D_param = jnp.full((D_INNER,), 0.1, jnp.float32)
        W_out = jax.random.normal(ks[7], (D_MODEL, D_INNER), jnp.float32) * 0.02
        residual_scale = jnp.asarray(0.3, jnp.float32)
        return dict(x=x, norm_w=norm_w, W_in=W_in, conv_w=conv_w, conv_b=conv_b, W_dt=W_dt, b_dt=b_dt, W_B=W_B, W_C=W_C, A_log=A_log, D_param=D_param, W_out=W_out, residual_scale=residual_scale)
    _L0_attn_in = _L0_attn_setup()

    def _L0_ffn_setup():
        import jax, jax.numpy as jnp
        import numpy as np
        B, S, D, H, E, K = (4, 512, 256, 1024, 8, 2)
        CAPACITY_FACTOR = 1.5
        C = int(CAPACITY_FACTOR * B * S * K / E)
        key = jax.random.key(seed)
        ks = jax.random.split(key, 6)
        x = jax.random.normal(ks[0], (B, S, D), dtype=jnp.float32)
        w_router = jax.random.normal(ks[1], (D, E), dtype=jnp.float32) * 0.02
        w1 = jax.random.normal(ks[2], (E, D, H), dtype=jnp.float32) * 0.02
        b1 = jnp.zeros((E, H), dtype=jnp.float32)
        w2 = jax.random.normal(ks[3], (E, H, D), dtype=jnp.float32) * 0.02
        b2 = jnp.zeros((E, D), dtype=jnp.float32)
        return {'x': x, 'w_router': w_router, 'w1': w1, 'b1': b1, 'w2': w2, 'b2': b2}
    _L0_ffn_in = _L0_ffn_setup()
    _d = {'L0_attn_x': _L0_attn_in['x'], 'L0_attn_norm_w': _L0_attn_in['norm_w'], 'L0_attn_W_in': _L0_attn_in['W_in'], 'L0_attn_conv_w': _L0_attn_in['conv_w'], 'L0_attn_conv_b': _L0_attn_in['conv_b'], 'L0_attn_W_dt': _L0_attn_in['W_dt'], 'L0_attn_b_dt': _L0_attn_in['b_dt'], 'L0_attn_W_B': _L0_attn_in['W_B'], 'L0_attn_W_C': _L0_attn_in['W_C'], 'L0_attn_A_log': _L0_attn_in['A_log'], 'L0_attn_D_param': _L0_attn_in['D_param'], 'L0_attn_W_out': _L0_attn_in['W_out'], 'L0_attn_residual_scale': _L0_attn_in['residual_scale'], 'L0_ffn_w_router': _L0_ffn_in['w_router'], 'L0_ffn_w1': _L0_ffn_in['w1'], 'L0_ffn_b1': _L0_ffn_in['b1'], 'L0_ffn_w2': _L0_ffn_in['w2'], 'L0_ffn_b2': _L0_ffn_in['b2']}
    _x0 = _d['L0_attn_x']
    _d['L0_attn_x'] = jax.random.normal(jax.random.fold_in(jax.random.key(seed), 1), (8, 1024, 256), dtype=_x0.dtype)
    del _x0
    return _d

def reference(L0_attn_x, L0_attn_norm_w, L0_attn_W_in, L0_attn_conv_w, L0_attn_conv_b, L0_attn_W_dt, L0_attn_b_dt, L0_attn_W_B, L0_attn_W_C, L0_attn_A_log, L0_attn_D_param, L0_attn_W_out, L0_attn_residual_scale, L0_ffn_w_router, L0_ffn_w1, L0_ffn_b1, L0_ffn_w2, L0_ffn_b2):

    def _L0_attn_ref(x, norm_w, W_in, conv_w, conv_b, W_dt, b_dt, W_B, W_C, A_log, D_param, W_out, residual_scale):
        import jax, jax.numpy as jnp
        import numpy as np
        D_MODEL = 256
        D_STATE = 16
        D_CONV = 4
        EXPAND = 2
        D_INNER = D_MODEL * EXPAND

        def soft_clamp(x, lo, hi, sharp):
            c = (hi + lo) / 2.0
            r = (hi - lo) / 2.0
            return jnp.tanh((x - c) / (r + 1e-08) * sharp) / sharp * r + c
        B, L, _ = x.shape
        var = jnp.mean(x * x, axis=-1, keepdims=True)
        xn = x * jax.lax.rsqrt(var + 1e-06) * norm_w
        proj = xn @ W_in.T
        x_branch, gate = (proj[..., :D_INNER], proj[..., D_INNER:])
        xc = jax.lax.conv_general_dilated(jnp.swapaxes(x_branch, 1, 2), conv_w, (1,), [(D_CONV - 1, 0)], dimension_numbers=('NCH', 'OIH', 'NCH'), feature_group_count=D_INNER)
        xc = xc + conv_b[None, :, None]
        xc = jnp.swapaxes(xc, 1, 2)
        xc = xc * jax.nn.sigmoid(xc)
        dt = soft_clamp(jax.nn.softplus(xc @ W_dt.T + b_dt), 0.001, 0.1, 0.5)
        Bp = xc @ W_B.T
        Cp = xc @ W_C.T
        A = -jnp.exp(soft_clamp(A_log, -5.0, 5.0, 0.5))
        dt_A = soft_clamp(dt[..., None] * A[None, None], -8.0, 8.0, 0.5)
        dA = jnp.exp(dt_A)
        dB = dt[..., None] * Bp[:, :, None, :]
        h0 = jnp.zeros((B, D_INNER, D_STATE), jnp.float32)

        def step(h, inp):
            dA_t, dB_t, x_t, C_t, t = inp
            h = h * dA_t + dB_t * x_t[:, :, None]
            nrm = jnp.sqrt(jnp.sum(h * h, axis=(1, 2), keepdims=True))
            fac = jnp.minimum(20.0 / (nrm + 1e-08), 1.0)
            h = jnp.where(t % 10 == 0, h * fac, h)
            y = jnp.einsum('bdn,bn->bd', h, C_t) + D_param * x_t
            return (h, y)
        xs = (jnp.swapaxes(dA, 0, 1), jnp.swapaxes(dB, 0, 1), jnp.swapaxes(xc, 0, 1), jnp.swapaxes(Cp, 0, 1), jnp.arange(L))
        _, ys = jax.lax.scan(step, h0, xs)
        x_ssm = jnp.swapaxes(ys, 0, 1)
        x_out = x_ssm * (gate * jax.nn.sigmoid(gate)) @ W_out.T
        scale = jax.nn.sigmoid(residual_scale) * 0.5
        return x + scale * x_out

    def _L0_ffn_ref(x, w_router, w1, b1, w2, b2):
        import jax, jax.numpy as jnp
        import numpy as np
        B, S, D, H, E, K = (4, 512, 256, 1024, 8, 2)
        CAPACITY_FACTOR = 1.5
        C = int(CAPACITY_FACTOR * B * S * K / E)
        Bs, Ss, Ds = x.shape
        N = Bs * Ss
        xf = x.reshape(N, Ds)
        logits = xf @ w_router
        probs = jax.nn.softmax(logits, axis=-1)
        gate, eidx = jax.lax.top_k(probs, K)
        gate = gate / jnp.sum(gate, axis=-1, keepdims=True)
        oh = jax.nn.one_hot(eidx, E, dtype=jnp.float32)
        ohf = oh.reshape(N * K, E)
        pos = jnp.cumsum(ohf, axis=0) - 1.0
        posk = jnp.sum(pos * ohf, axis=-1).reshape(N, K).astype(jnp.int32)
        keep = posk < C
        gate = gate * keep.astype(gate.dtype)
        e_flat = eidx.reshape(-1)
        p_flat = jnp.where(keep, posk, 0).reshape(-1)
        contrib = (xf[:, None, :] * keep[..., None].astype(xf.dtype)).reshape(N * K, Ds)
        expert_in = jnp.zeros((E, C, Ds), dtype=xf.dtype).at[e_flat, p_flat].add(contrib)
        h = jax.nn.relu(jnp.einsum('ecd,edh->ech', expert_in, w1) + b1[:, None, :])
        expert_out = jnp.einsum('ech,eho->eco', h, w2) + b2[:, None, :]
        tok = expert_out[e_flat, p_flat].reshape(N, K, -1)
        y = jnp.sum(tok * gate[..., None], axis=1)
        return y.reshape(Bs, Ss, -1)
    x = L0_attn_x
    x = _layernorm(x + _L0_attn_ref(x, L0_attn_norm_w, L0_attn_W_in, L0_attn_conv_w, L0_attn_conv_b, L0_attn_W_dt, L0_attn_b_dt, L0_attn_W_B, L0_attn_W_C, L0_attn_A_log, L0_attn_D_param, L0_attn_W_out, L0_attn_residual_scale), axis=-1)
    x = _layernorm(x + _L0_ffn_ref(x, L0_ffn_w_router, L0_ffn_w1, L0_ffn_b1, L0_ffn_w2, L0_ffn_b2), axis=-1)
    return x

_drawn_inputs = setup_inputs


def setup_inputs(seed=0):
    import zlib

    import numpy as np

    out = dict(_drawn_inputs(seed))
    spreads = {'L0_attn_norm_w': (1.0, 0.6),
     'L0_attn_conv_b': (0.0, 0.8),
     'L0_attn_b_dt': (-2.0, 0.6),
     'L0_attn_D_param': (0.10000000149011612, 0.6),
     'L0_ffn_b1': (0.0, 0.409),
     'L0_ffn_b2': (0.0, 0.1)}
    factors = {'L0_attn_W_in': 8.0,
     'L0_attn_conv_w': 8.0,
     'L0_attn_W_dt': 8.0,
     'L0_attn_W_B': 8.0,
     'L0_attn_W_C': 8.0,
     'L0_attn_A_log': 8.0,
     'L0_attn_W_out': 8.0}
    for name, (base, spread) in spreads.items():
        noise = np.random.default_rng([zlib.crc32(name.encode()), seed]).standard_normal(out[name].shape)
        drawn = base * np.exp(spread * noise) if base else spread * noise
        out[name] = jnp.asarray(drawn.astype(out[name].dtype))
    for name, factor in factors.items():
        out[name] = (out[name] * factor).astype(out[name].dtype)
    return out
```

```python
import numpy as np
import concourse.bass as bass
from concourse import mybir
from contextlib import ExitStack

F32 = mybir.dt.float32
I32 = mybir.dt.int32
U32 = mybir.dt.uint32
ALU = mybir.AluOpType
ACT = mybir.ActivationFunctionType
AX = mybir.AxisListType

B, L, DM, DI, NS = 8, 1024, 256, 512, 16
E, HF, CAP = 8, 1024, 768
T = 20
NB = 52
LP = NB * T
NC = 2 * NB
CH = 704


class Queue:

    def __init__(self):
        self.items = []

    def play(self, eng):
        seen = {}
        for waits, fn, sem, inc in self.items:
            for s, v in waits:
                if seen.get(s, 0) < v:
                    eng.wait_ge(s.h, v)
                    seen[s] = v
            if fn is None:
                continue
            ins = fn()
            if sem is not None:
                ins.then_inc(sem.h, inc)


class Sem:

    def __init__(self, h):
        self.h, self.n = h, 0


def put(q, fn, waits=(), sem=None, dma=False):
    inc = 16 if dma else 1
    tok = None
    if sem is not None:
        sem.n += inc
        tok = (sem, sem.n)
    q.items.append(([w for w in waits if w is not None], fn, sem, inc))
    return tok


def run_block(nc, qs):
    with nc.Block() as block:
        @block.sync
        def _(eng):
            qs["sp"].play(eng)

        @block.scalar
        def _(eng):
            qs["act"].play(eng)

        @block.vector
        def _(eng):
            qs["dve"].play(eng)

        @block.gpsimd
        def _(eng):
            qs["pool"].play(eng)

        @block.tensor
        def _(eng):
            qs["pe"].play(eng)


def ssm_phase(nc, d, XE, X2d, LGd, Bd, Cd):
    ctx = ExitStack()
    with ctx:
        def sb(name, shape, dt=F32):
            return ctx.enter_context(nc.sbuf_tensor(name, shape, dt))

        sems = {}

        def sem(name):
            if name not in sems:
                sems[name] = Sem(ctx.enter_context(nc.semaphore(name)))
            return sems[name]

        qs = {k: Queue() for k in ("sp", "act", "dve", "pool", "pe")}
        SP, AC, DV, PO, PE = qs["sp"], qs["act"], qs["dve"], qs["pool"], qs["pe"]
        V, S, G, M, Y = nc.vector, nc.scalar, nc.gpsimd, nc.tensor, nc.sync

        DA = sb("DA", [128, 4, 8, 4, 16, 11])
        H = sb("H", [128, 3, 4, CH])
        BB = sb("BB", [128, 3, 16, 4, 10])
        CB = sb("CB", [128, 3, 16, 4, 10])
        WIN = sb("WIN", [128, 2, 1024])
        WDT = sb("WDT", [128, 4, 512])
        WBC = sb("WBC", [128, 4, 64])
        WO = sb("WO", [128, 4, 256])
        WR = sb("WR", [128, 2, 8])
        ID = sb("ID", [128, 128])
        ONE = sb("ONE", [128, 128])
        MEAN = sb("MEAN", [128, 128])
        AS = sb("AS", [128, 4, 16])
        CW = sb("CW", [128, 4, 4])
        PV = sb("PV", [128, 3, 4])
        NW = sb("NW", [128, 2])
        SC = sb("SC", [128, 2])
        CST = sb("CST", [128, 4])
        XT = sb("XT", [128, 2, 2, 160])
        XN = sb("XN", [128, 2, 2, 160])
        RST = sb("RST", [128, 160])
        XB = sb("XB", [128, 4, 8, 23])
        TA = sb("TA", [128, 4, 8, 20])
        TB = sb("TB", [128, 4, 8, 20])
        XC = sb("XC", [128, 2, 4, 8, 20])
        DT = sb("DT", [128, 2, 4, 8, 20])
        SG = sb("SG", [128, 2, 4, 8, 21])
        DX = sb("DX", [128, 2, 4, 8, 21])
        Z = sb("Z", [128, 4, 8, 20])
        BS = sb("BS", [16, 2, 8, 10])
        CS = sb("CS", [64, 4, 8, 10])
        XR = sb("XR", [80, 2, 256])
        VV = sb("VV", [80, 2, 256])
        BN = sb("BN", [80, 2, 6])
        MVR = sb("MVR", [80, 2, 2])
        SD = sb("SD", [80, 2])
        X2T = sb("X2T", [128, 4, 80])
        LGS = sb("LGS", [80, 2, 8])
        SS = sb("SS", [128, 2, 4])
        JK = sb("JK", [128, 64])
        FW = sb("FW", [128, 2, 4, 4])
        FI = sb("FI", [128, 2, 4], I32)
        FC = sb("FC", [128, 2, 4])
        PM = ctx.enter_context(nc.psum_tensor("PM", [128, 2048], F32))
        PB = [ctx.enter_context(nc.psum_tensor(f"PB{i}", [128, 512], F32)) for i in range(2)]

        YB = [ctx.enter_context(nc.psum_tensor(f"YB{i}", [128, 512], F32)) for i in range(2)]

        def U(c):
            return PM[:, 320 * (c % 2):320 * (c % 2) + 320].rearrange("p (a b t) -> p a b t", a=4, b=8)

        def DBX(u):
            return PM[:, 640 + CH * (u % 2):640 + CH * (u % 2) + CH]

        def YP(q):
            return YB[q % 2][:, 0:160]

        def NP(g):
            return YB[g][:, 256:260]

        w = []
        for k, (dst, src) in enumerate([
                (WIN[:], d["w_in"].rearrange("(a p) n -> p a n", p=128)),
                (WDT[:], d["w_dt"].rearrange("(a p) n -> p a n", p=128)),
                (WBC[:], d["w_bc"].rearrange("(a p) n -> p a n", p=128)),
                (WO[:], d["w_out"].rearrange("(a p) n -> p a n", p=128)),
                (WR[:], d["w_router"].rearrange("(a p) n -> p a n", p=128)),
                (ID[:], d["ident"]),
                (AS[:], d["a_log"].rearrange("(a p) n -> p a n", p=128)),
                (CW[:], d["conv_w"].rearrange("(a p) n -> p a n", p=128)),
                (PV[:], d["vecs"]),
                (NW[:], d["norm_w"]),
                (SC[:, 0:1], d["res"].to_broadcast([128, 1])),
        ]):
            w.append(put(AC, lambda dst=dst, src=src: S.dma_start(dst, src), (), sem("w_load"), dma=True))
        wall = w[-1]
        s_pre = sem("pre")
        c1 = put(DV, lambda: V.memset(ONE[:], 1.0), (), s_pre)
        c1 = put(DV, lambda: V.memset(MEAN[:], 1.0 / 256), (), s_pre)
        KD = 0.5 / (0.0495 + 1e-8)
        for col, val in enumerate((1e-6, 1e-5, -0.0505 * KD, 0.0)):
            c1 = put(DV, lambda col=col, val=val: V.memset(CST[:, col:col + 1], val), (), s_pre)
        c1 = put(DV, lambda: V.memset(XB[:], 0.0), (), s_pre)
        c1 = put(DV, lambda: V.memset(CS[:], 0.0), (), s_pre)
        c1 = put(DV, lambda: V.memset(SG[:], 0.0), (), s_pre)
        c1 = put(DV, lambda: V.memset(DX[:], 0.0), (), s_pre)
        c1 = put(DV, lambda: V.memset(DA[:, :, :, :, :, 0:1].rearrange("p c b a n t -> p (c b a n) t"), 0.0), (), s_pre)
        z0 = put(PO, lambda: G.memset(H[:], 0.0), (), sem("h0"))
        ze = None
        ROWS = H[:].rearrange("p a b c -> p (a b c)")
        for k in range(2):
            dst = XE[k * 3072:(k + 1) * 3072, :].rearrange("(p r) n -> p (r n)", p=128)
            ze = put(SP, lambda dst=dst: Y.dma_start(dst, ROWS[:, 0:6144]), (z0,), sem("xe0"), dma=True)
        c1 = put(DV, lambda: V.tensor_scalar(CW[:], CW[:], 0.5, None, ALU.mult), (wall,), s_pre)
        c1 = put(DV, lambda: V.tensor_scalar(PV[:, 0, :], PV[:, 0, :], 0.5, None, ALU.mult), (), s_pre)
        a1 = put(AC, lambda: S.activation(AS[:], AS[:], ACT.Tanh, scale=0.5 / (5.0 + 1e-8)), (wall,), sem("pre_a"))
        a1 = put(AC, lambda: S.activation(AS[:], AS[:], ACT.Exp, scale=10.0), (a1,), sem("pre_a"))
        c1 = put(DV, lambda: V.tensor_scalar(AS[:], AS[:], -0.5 / (8.0 + 1e-8), None, ALU.mult), (a1,), s_pre)
        a1 = put(AC, lambda: S.activation(SC[:, 1:2], SC[:, 0:1], ACT.Tanh, scale=0.5), (), sem("pre_a"))
        c1 = put(DV, lambda: V.tensor_scalar(SC[:, 0:1], SC[:, 1:2], 0.125, 0.125, ALU.mult, ALU.add), (a1,), s_pre)
        pre = put(DV, lambda: V.tensor_scalar(WO[:], WO[:], SC[:, 0:1], None, ALU.mult), (c1,), s_pre)

        k = {}
        bank_free = [[], []]
        nbank = [0]

        def bank():
            n = nbank[0] % 2
            nbank[0] += 1
            waits, bank_free[n] = bank_free[n], []
            return n, PB[n], waits

        def mms(specs, waits, s):
            tok = None
            for n, (o, l, r, st, sp) in enumerate(specs):
                tok = put(PE, lambda o=o, l=l, r=r, st=st, sp=sp: M.matmul(o, l, r, start=st, stop=sp),
                          waits if n == 0 else (), s if n == len(specs) - 1 else None)
            return tok

        def ok(j):
            return 0 <= j < NB

        def load_x(j):
            if ok(j):
                k["xt", j] = put(SP, lambda: Y.dma_start(XT[:, j % 2], d["xT"][j]),
                                 (k.get(("xn", j - 2)), k.get(("sq", j - 2))), sem(f"xt{j % 2}"), dma=True)

        def squares(j):
            if ok(j):
                k["sq", j] = put(AC, lambda: S.activation(TB[:].rearrange("p a b t -> p (a b t)")[:, 0:320],
                                                          XT[:, j % 2].rearrange("p a t -> p (a t)"), ACT.Square),
                                 (k["xt", j], k.get(("xc", j - 1))), sem("sq"))

        def sum_squares(j):
            if ok(j):
                n, p, waits = bank()
                sq = TB[:].rearrange("p a b t -> p (a b t)")
                k["ssum", j] = mms([(p[:, 0:160], MEAN[:], sq[:, 0:160], True, False),
                                    (p[:, 0:160], MEAN[:], sq[:, 160:320], False, True)],
                                   [k["sq", j], pre] + waits, sem("ssum"))
                k["rt", j] = (n, p)

        def roots(j):
            if ok(j):
                n, p = k["rt", j]
                k["root", j] = put(AC, lambda: S.activation(RST[:], p[:, 0:160], ACT.Sqrt, bias=CST[:, 0:1]),
                                   (k["ssum", j], k.get(("xn", j - 1)), pre), sem("root"))
                bank_free[n].append(k["root", j])

        def normed(j):
            if ok(j):
                r = put(DV, lambda: V.reciprocal(RST[:], RST[:]), (k["root", j],), sem("rs"))
                for a in range(2):
                    k["xn", j] = put(DV, lambda a=a: V.scalar_tensor_tensor(
                        XN[:, j % 2, a], XT[:, j % 2, a], NW[:, a:a + 1], RST[:], ALU.mult, ALU.mult),
                        (r, k.get(("gate", j - 2))), sem("xn"))

        def halo(j):
            if ok(j) and j > 0:
                k["halo", j] = put(DV, lambda: V.tensor_copy(XB[:, :, :, 0:3], XB[:, :, :, 20:23]),
                                   (k["conv", j - 1],), sem("halo"))

        def project(j, first, name):
            if not ok(j):
                return
            out = []
            for m in range(2):
                n, p, waits = bank()
                sp = []
                for a in range(2):
                    c = first + 256 * m + 128 * a
                    for kk in range(2):
                        sp.append((p[:, 160 * a:160 * a + 160], WIN[:, kk, c:c + 128], XN[:, j % 2, kk],
                                   kk == 0, kk == 1))
                tok = mms(sp, [k["xn", j]] + waits, sem("proj"))
                out.append((n, p, tok))
            k[name, j] = tok
            k[name + "_b", j] = out

        def branch_out(j):
            if ok(j):
                for m, (n, p, tok) in enumerate(k["br_b", j]):
                    k["xb", j] = put(AC, lambda m=m, p=p: S.activation(
                        XB[:, 2 * m:2 * m + 2, :, 3:23], p[:, 0:320].rearrange("p (a b t) -> p a b t", a=2, b=8),
                        ACT.Copy), (tok, k.get(("halo", j)), k.get(("conv", j - 1)), pre), sem("xb"))
                    bank_free[n].append(k["xb", j])

        def conv(j, part):
            if not ok(j):
                return
            for tap in (2 * part, 2 * part + 1):
                toks = []
                for a in range(4):
                    if tap == 0:
                        toks.append(put(DV, lambda a=a: V.tensor_scalar(
                            TA[:, a], XB[:, a, :, 0:20], CW[:, a, 0:1], PV[:, 0, a:a + 1], ALU.mult, ALU.add),
                            (k["xb", j], k.get(("dt", j - 1))), sem("conv")))
                    else:
                        toks.append(put(DV, lambda a=a, tap=tap: V.scalar_tensor_tensor(
                            TA[:, a], XB[:, a, :, tap:tap + 20], CW[:, a, tap:tap + 1], TA[:, a],
                            ALU.mult, ALU.add), (k["cv", j][a],), sem("conv")))
                k["cv", j] = toks
            k["conv", j] = toks[-1]

        def silu_tanh(j):
            if ok(j):
                k["th", j] = put(AC, lambda: S.activation(TB[:], TA[:], ACT.Tanh),
                                 (k["conv", j], k.get(("sg", j - 1))), sem("th"))

        def silu(j):
            if ok(j):
                k["xc", j] = put(DV, lambda: V.scalar_tensor_tensor(
                    XC[:, j % 2].rearrange("p a b t -> p (a b t)"), TB[:].rearrange("p a b t -> p (a b t)"), 1.0,
                    TA[:].rearrange("p a b t -> p (a b t)"), ALU.add, ALU.mult),
                    (k["th", j], k.get(("bc", j - 2)), k.get(("dx", j - 2)), k.get(("u", 2 * j - 3))), sem("xc"))

        def dt_proj(j):
            if not ok(j):
                return
            out = []
            for m in range(2):
                n, p, waits = bank()
                sp = []
                for a in range(2):
                    c = 256 * m + 128 * a
                    for kk in range(4):
                        sp.append((p[:, 160 * a:160 * a + 160], WDT[:, kk, c:c + 128],
                                   XC[:, j % 2, kk].rearrange("p b t -> p (b t)"), kk == 0, kk == 3))
                out.append((n, p, mms(sp, [k["xc", j]] + waits, sem("dtp"))))
            k["dtp", j] = out

        def bc_proj(j):
            if not ok(j):
                return
            n, p, waits = bank()
            k["bc", j] = mms([(p[0:64, 0:160], WBC[:, kk, :], XC[:, j % 2, kk].rearrange("p b t -> p (b t)"),
                               kk == 0, kk == 3) for kk in range(4)], waits, sem("bcp"))
            k["bcb", j] = (n, p)

        def dt_bias(j):
            if not ok(j):
                return
            for m, (n, p, tok) in enumerate(k["dtp", j]):
                for a in range(2):
                    k["dtb", j] = put(DV, lambda m=m, a=a, p=p: V.tensor_scalar(
                        TA[:, 2 * m + a].rearrange("p b t -> p (b t)"), p[:, 160 * a:160 * a + 160],
                        PV[:, 1, 2 * m + a:2 * m + a + 1], None, ALU.add), (tok,), sem("dtb"))
                bank_free[n].append(k["dtb", j])

        def bc_out(j):
            if not ok(j):
                return
            n, p = k["bcb", j]
            pv = p[:, 0:160].rearrange("p (b c t) -> p c b t", b=8, c=2)
            b = put(AC, lambda: S.activation(BS[:], pv[0:16], ACT.Copy),
                    (k["bc", j], k.get(("bd", j - 1))), sem("bcs"))
            q0 = (2 * j) % 4
            put(AC, lambda: S.activation(CS[32:48, q0:q0 + 2, :, 1:10], pv[32:48, :, :, 0:9], ACT.Copy),
                (k.get(("cd", j - 2)), pre), sem("bcs"))
            put(AC, lambda: S.activation(CS[32:48, q0 + 1, :, 0:1], pv[32:48, 0, :, 9:10], ACT.Copy),
                (), sem("bcs"))
            c = put(AC, lambda: S.activation(CS[32:48, (q0 + 2) % 4, :, 0:1], pv[32:48, 1, :, 9:10], ACT.Copy),
                    (k.get(("cd", j - 1)),), sem("bcs"))
            bank_free[n].append(c)
            cw_ = 4 * 10
            for gg in range(2):
                k["bd", j] = put(SP, lambda gg=gg: Y.dma_start(
                    Bd[2 * j:2 * j + 2, gg].rearrange("c n e -> n c e"),
                    BS[:, :, 4 * gg:4 * gg + 4, :].rearrange("n c b t -> n c (b t)")), (b,), sem(f"bd{j % 2}"), dma=True)
                k["cd", j] = put(SP, lambda gg=gg: Y.dma_start(
                    Cd[2 * j:2 * j + 2, gg].rearrange("c n e -> n c e"),
                    CS[32:48, q0:q0 + 2, 4 * gg:4 * gg + 4, :].rearrange("n c b t -> n c (b t)")),
                    (c,), sem(f"cd{j % 2}"), dma=True)

        def softplus_log(j):
            if not ok(j):
                return
            t = put(AC, lambda: S.activation(TB[:], TA[:], ACT.Abs),
                    (k["dtb", j], k["xc", j], k.get(("ssum", j + 1))), sem("sp"))
            t = put(AC, lambda: S.activation(TB[:], TB[:], ACT.Exp, scale=-1.0), (t,), sem("sp"))
            k["ln", j] = put(AC, lambda: S.activation(TB[:], TB[:], ACT.Ln, bias=ONE[:, 0:1]), (t,), sem("sp"))

        def softplus(j):
            if ok(j):
                k["spl", j] = put(DV, lambda: V.scalar_tensor_tensor(
                    TA[:].rearrange("p a b t -> p (a b t)"), TA[:].rearrange("p a b t -> p (a b t)"), 0.0,
                    TB[:].rearrange("p a b t -> p (a b t)"), ALU.max, ALU.add), (k["ln", j],), sem("spl"))

        def dt_tanh(j):
            if ok(j):
                k["dth", j] = put(AC, lambda: S.activation(TA[:], TA[:], ACT.Tanh, bias=CST[:, 2:3], scale=KD),
                                  (k["spl", j],), sem("dth"))

        def dt_out(j):
            if ok(j):
                k["dt", j] = put(DV, lambda: V.tensor_scalar(DT[:, j % 2], TA[:], 0.0495 / 0.5, 0.0505, ALU.mult, ALU.add),
                                 (k["dth", j], k.get(("z64", j - 2)), k.get(("u", 2 * j - 3))), sem("dt"))

        def dt_x(c):
            j, cc = c // 2, c % 2
            t = slice(10 * cc, 10 * cc + 10)
            k["u", c] = put(DV, lambda: V.tensor_tensor(U(c), DT[:, j % 2, :, :, t], XC[:, j % 2, :, :, t], ALU.mult),
                            (k["dt", j], k["xc", j], k.get(("m1", 2 * (c - 2) + 1))), sem("u"))
            if c == 0:
                k["u", c] = put(DV, lambda: V.memset(U(0).rearrange("p a b t -> p (a b) t")[:, :, 0:9], 0.0),
                                (k["u", c],), sem("u"))

        def gate_tanh(j):
            if ok(j):
                for m, (n, p, tok) in enumerate(k["gate_b", j]):
                    k["tg", j] = put(AC, lambda m=m, p=p: S.activation(
                        TB[:, 2 * m:2 * m + 2].rearrange("p a b t -> p (a b t)"), p[:, 0:320], ACT.Tanh, scale=0.5),
                        (tok, k.get(("spl", j))), sem("tg"))

        def gate(j):
            if not ok(j):
                return
            if j > 0:
                put(DV, lambda: V.tensor_copy(SG[:, j % 2, :, :, 0:1], SG[:, 1 - j % 2, :, :, 20:21]),
                    (k["sg", j - 1], k.get(("z", 4 * j - 5))), sem("sg"))
            for m, (n, p, tok) in enumerate(k["gate_b", j]):
                for a in range(2):
                    k["sg", j] = put(DV, lambda m=m, a=a, p=p: V.scalar_tensor_tensor(
                        SG[:, j % 2, 2 * m + a, :, 1:21], TB[:, 2 * m + a], 1.0,
                        p[:, 160 * a:160 * a + 160].rearrange("p (b t) -> p b t", b=8), ALU.add, ALU.mult),
                        (k["tg", j],), sem("sg"))
                bank_free[n].append(k["sg", j])

        def gate_d(j):
            if not ok(j):
                return
            if j > 0:
                put(DV, lambda: V.tensor_copy(DX[:, j % 2, :, :, 0:1], DX[:, 1 - j % 2, :, :, 20:21]),
                    (k["dx", j - 1],), sem("dx"))
            for a in range(4):
                k["dx", j] = put(DV, lambda a=a: V.scalar_tensor_tensor(
                    DX[:, j % 2, a, :, 1:21], XC[:, j % 2, a], PV[:, 2, a:a + 1], SG[:, j % 2, a, :, 1:21],
                    ALU.mult, ALU.mult), (k["sg", j],), sem("dx"))

        def decay_tanh(j, n0, n1):
            if not ok(j):
                return
            for n in range(n0, min(n1, 64)):
                a, s = n // 16, n % 16
                c0 = (2 * j) % 4
                k["z64", j] = put(AC, lambda a=a, s=s: S.activation(
                    DA[:, c0:c0 + 2, :, a, s, 1:11].rearrange("p c b t -> p b c t"),
                    DT[:, j % 2, a].rearrange("p b (c t) -> p b c t", c=2), ACT.Tanh, scale=AS[:, a, s:s + 1]),
                    (k["dt", j], k.get(("scan", 4 * (j - 2) + 3)), pre), sem("z64"))

        def decay_exp(j, r):
            if ok(j):
                c, g = r // 2, r % 2
                v = DA[:, (2 * j + c) % 4, 4 * g:4 * g + 4].rearrange("p b a n t -> p (b a n) t")[:, :, 1:11]
                k["da", 4 * j + r] = put(AC, lambda: S.activation(v, v, ACT.Exp, scale=16.0),
                                         (k["z64", j],), sem("da"))

        def bring(q):
            if 0 <= q < 2 * NC:
                c, g = q // 2, q % 2
                j = c // 2
                k["bb", q] = put(SP, lambda: Y.dma_start(
                    BB[:, q % 3].rearrange("p n b t -> p (n b t)"),
                    Bd[c, g].rearrange("n e -> (n e)").partition_broadcast(128)),
                    (k["bd", j], k.get(("m1", q - 3))), sem(f"bb{q % 3}"), dma=True)
                k["cb", q] = put(SP, lambda: Y.dma_start(
                    CB[:, q % 3].rearrange("p n b t -> p (n b t)"),
                    Cd[c, g].rearrange("n e -> (n e)").partition_broadcast(128)),
                    (k["cd", j], k.get(("hc", q - 3))), sem(f"cb{q % 3}"), dma=True)

        def factor(q):
            c, g = q // 2, q % 2
            s = sem("fac")
            sq, y, n, w = FW[:, g, 0], FW[:, g, 1], FW[:, g, 2], FW[:, g, 3]
            t = put(DV, lambda: V.tensor_scalar(sq, NP(g), 1e-30, None, ALU.max), (k["nrm", q - 2], k.get(("ca", q - 2))), s)
            k["nread", q - 2] = t
            t = put(DV, lambda: V.tensor_scalar(FI[:, g], sq.bitcast(I32), 1, None, ALU.logical_shift_right),
                    (t,), s)
            t = put(DV, lambda: V.tensor_scalar(y.bitcast(I32), FI[:, g], -1, 0x5f3759df, ALU.mult, ALU.add),
                    (t,), s)
            t = put(DV, lambda: V.tensor_tensor(n, sq, y, ALU.mult), (t,), s)
            t = put(DV, lambda: V.tensor_scalar(y, y, -0.5, None, ALU.mult), (t,), s)
            for it in range(3):
                t = put(DV, lambda: V.tensor_tensor(w, n, y, ALU.mult), (t,), s)
                t = put(DV, lambda: V.scalar_tensor_tensor(n, w, 1.5, n, ALU.add, ALU.mult), (t,), s)
                if it < 2:
                    t = put(DV, lambda: V.scalar_tensor_tensor(y, w, 1.5, y, ALU.add, ALU.mult), (t,), s)
            t = put(DV, lambda: V.tensor_scalar(n, n, 1e-8, None, ALU.add), (t,), s)
            t = put(DV, lambda: V.reciprocal(n, n), (t,), s)
            k["fac", q] = put(DV, lambda: V.tensor_scalar(FC[:, g], n, 20.0, 1.0, ALU.mult, ALU.min), (t,), s)

        def mult(q, u):
            c, g = q // 2, q % 2
            j, cc, b = c // 2, c % 2, 4 * g + u
            o = DBX(u).rearrange("p (a n t) -> p a n t", a=4, n=16)[:, :, :, 1:11]
            i0 = U(c)[:, :, b, :].unsqueeze(2).to_broadcast([128, 4, 16, 10])
            i1 = BB[:, q % 3, :, u, :].unsqueeze(1).to_broadcast([128, 4, 16, 10])
            k["m1", q] = put(DV, lambda: V.tensor_tensor(o, i0, i1, ALU.mult), (k["bb", q], k["u", c]), sem("m1"))

        def carry(q, u):
            o = DBX(u).rearrange("p (a t) -> p a t", t=11)[:, :, 0]
            if q < 2:
                k["ca", q] = put(DV, lambda: V.memset(o, 0.0), (), sem("ca"))
                return
            i = H[:, (q - 2) % 3, u].rearrange("p (a t) -> p a t", t=11)[:, :, 10]
            k["ca", q] = put(DV, lambda: V.tensor_scalar(o, i, FC[:, q % 2, u:u + 1], None, ALU.mult),
                             (k["fac", q],), sem("ca"))

        def scan(q, u):
            c, g = q // 2, q % 2
            a0 = DA[:, c % 4, 4 * g + u].rearrange("p a n t -> p (a n t)")
            k["scan", q] = put(DV, lambda: V.tensor_tensor_scan(
                H[:, q % 3, u], a0, DBX(u), 0.0, ALU.mult, ALU.add),
                (k["m1", q], k["ca", q], k["da", q], k.get(("ys", q - 3)), ze if q < 3 else None), sem("scan"))
            k["scan", q, u] = k["scan", q]

        def squared(q, u):
            g = q % 2
            h = H[:, q % 3, u].rearrange("p (a t) -> p a t", t=11)[:, :, 10]
            k["sqs", q] = put(DV, lambda: V.tensor_tensor_reduce(
                out=JK[:], in0=h, in1=h, scale=1.0, scalar=0.0, op0=ALU.mult, op1=ALU.add,
                accum_out=SS[:, g, u:u + 1]), (k["scan", q, u], k.get(("nrm", q - 2)), k.get("jk")), sem("sqs"))
            k["jk"] = k["sqs", q]

        def hc(q, u):
            h = H[:, q % 3, u].rearrange("p (a n t) -> p a n t", a=4, n=16)[:, :, :, 0:10]
            i1 = CB[:, q % 3, :, u, :].unsqueeze(1).to_broadcast([128, 4, 16, 10])
            k["hc", q] = put(PO, lambda: G.tensor_tensor(h, h, i1, ALU.mult),
                             (k["scan", q, u], k["cb", q]), sem("hc"))

        def norm_sum(q):
            k["nrm", q] = mms([(NP(q % 2), ONE[:], SS[:, q % 2], True, True)],
                              (k["sqs", q], k.get(("nread", q - 2)), k.get(("z", q - 2))), sem("nrm"))

        def y_sum(q):
            if not 0 <= q < 2 * NC:
                return
            hv = H[:, q % 3].rearrange("p u (a n t) -> p u a n t", a=4, n=16)
            k["ys", q] = mms([(YP(q).rearrange("p (u a t) -> p u a t", u=4, a=4), ID[:], hv[:, :, :, n, 0:10],
                               n == 0, n == 15) for n in range(16)],
                             (k["hc", q], k.get(("z", q - 2)), k.get(("nread", q))), sem("ys"))

        def z_out(q):
            if not 0 <= q < 2 * NC:
                return
            c, g = q // 2, q % 2
            j, cc = c // 2, c % 2

            def vw(t):
                return t.rearrange("p a b t -> p b a t")
            o = vw(Z[:, :, 4 * g:4 * g + 4, 10 * cc:10 * cc + 10])
            yv = YP(q).rearrange("p (u a t) -> p u a t", u=4, a=4)
            t = put(DV, lambda: V.tensor_tensor(
                o, yv, vw(SG[:, j % 2, :, 4 * g:4 * g + 4, 10 * cc:10 * cc + 10]), ALU.mult),
                (k["ys", q], k.get(("op", j - 1)), k["sg", j]), sem("zm"))
            k["z", q] = put(DV, lambda: V.tensor_tensor(
                o, o, vw(DX[:, j % 2, :, 4 * g:4 * g + 4, 10 * cc:10 * cc + 10]), ALU.add),
                (t, k["dx", j]), sem("z"))

        def load_res(i):
            if ok(i):
                for g in range(2):
                    for b in range(4):
                        k["xr", i] = put(SP, lambda g=g, b=b: Y.dma_start(
                            XR[20 * b:20 * b + 20, g, :], d["xp"][4 * g + b, T * i:T * i + T, :]),
                            (k.get(("v", i - 1)),), sem("xr"), dma=True)

        def out_proj(i):
            if ok(i):
                n, p, waits = bank()
                zf = Z[:].rearrange("p a b t -> p a (b t)")
                k["op", i] = mms([(p[0:80, 256 * g:256 * g + 256], zf[:, a, 80 * g:80 * g + 80], WO[:, a, :],
                                   a == 0, a == 3) for g in range(2) for a in range(4)],
                                 [k["z", 4 * i + 3], pre] + waits, sem("op"))
                k["opb", i] = (n, p)

        def residual(i):
            if ok(i):
                n, p = k["opb", i]
                k["v", i] = put(DV, lambda: V.scalar_tensor_tensor(
                    VV[:].rearrange("p a b -> p (a b)"), XR[:].rearrange("p a b -> p (a b)"), 2.0, p[0:80, :],
                    ALU.mult, ALU.add), (k["op", i], k["xr", i], k.get(("x2d", i - 1)), k.get(("tr", i - 1))),
                    sem("v"))
                bank_free[n].append(k["v", i])
                for g in range(2):
                    t = put(DV, lambda g=g: V.bn_stats(BN[:, g], VV[:, g]), (k["v", i],), sem("bn"))
                for g in range(2):
                    k["mv", i] = put(DV, lambda g=g: V.bn_aggr(MVR[:, g], BN[:, g]), (t,), sem("mv"))

        def ln_root(i):
            if ok(i):
                k["sd", i] = put(AC, lambda: S.activation(SD[:], MVR[:, :, 1], ACT.Sqrt, bias=CST[0:80, 1:2]),
                                 (k["mv", i], k.get(("x2", i - 1))), sem("sd"))

        def ln_out(i):
            if ok(i):
                t = put(DV, lambda: V.reciprocal(SD[:], SD[:]), (k["sd", i],), sem("rsd"))
                for g in range(2):
                    k["x2", i] = put(DV, lambda g=g: V.tensor_scalar(
                        VV[:, g], VV[:, g], MVR[:, g, 0:1], SD[:, g:g + 1], ALU.subtract, ALU.mult),
                        (t,), sem("x2"))
                for g in range(2):
                    for b in range(4):
                        k["x2d", i] = put(SP, lambda g=g, b=b: Y.dma_start(
                            X2d[4 * g + b, T * i:T * i + T, :], VV[20 * b:20 * b + 20, g, :]),
                            (k["x2", i],), sem("x2d"), dma=True)

        def transposed(i):
            if ok(i):
                n, p, waits = bank()
                tok = None
                for g in range(2):
                    for a in range(2):
                        o = p[:, 80 * (2 * g + a):80 * (2 * g + a) + 80]
                        tok = put(PE, lambda o=o, g=g, a=a: M.transpose(
                            o, VV[:, g, 128 * a:128 * a + 128], ID[0:80, 0:80]),
                            [k["x2", i]] + waits if (g, a) == (0, 0) else (), sem("tr"))
                k["tr", i] = tok
                k["x2t", i] = put(AC, lambda: S.activation(X2T[:].rearrange("p a b -> p (a b)"), p[:, 0:320],
                                                           ACT.Copy), (tok, k.get(("lg", i - 1))), sem("x2t"))
                bank_free[n].append(k["x2t", i])

        def logits(i):
            if ok(i):
                n, p, waits = bank()
                k["lg", i] = mms([(p[0:80, 8 * g:8 * g + 8], X2T[:, 2 * g + a, :], WR[:, a, :], a == 0, a == 1)
                                  for g in range(2) for a in range(2)], [k["x2t", i]] + waits, sem("lg"))
                t = put(DV, lambda: V.tensor_copy(LGS[:].rearrange("p a b -> p (a b)"), p[0:80, 0:16]),
                        (k["lg", i], k.get(("lgd", i - 1))), sem("lgs"))
                bank_free[n].append(t)
                for g in range(2):
                    for b in range(4):
                        k["lgd", i] = put(SP, lambda g=g, b=b: Y.dma_start(
                            LGd[4 * g + b, T * i:T * i + T, :], LGS[20 * b:20 * b + 20, g, :]),
                            (t,), sem("lgd"), dma=True)

        def window(i):
            live = ok(i)
            for s in range(16):
                r, u = s // 4, s % 4
                q = 4 * i + r
                if s == 0:
                    load_x(i + 4)
                    project(i + 2, 0, "br")
                    halo(i + 2)
                if s == 1:
                    branch_out(i + 2)
                if s == 2:
                    conv(i + 2, 0)
                if s == 3:
                    conv(i + 2, 1)
                    project(i + 1, 512, "gate")
                if s == 4:
                    gate_tanh(i + 1)
                if s == 6:
                    gate(i + 1)
                    out_proj(i - 1)
                if s == 7:
                    gate_d(i + 1)
                    silu_tanh(i + 2)
                    residual(i - 1)
                    if live:
                        dt_x(2 * i + 1)
                if s == 8:
                    silu(i + 2)
                    load_res(i)
                if s == 9:
                    dt_proj(i + 2)
                    squares(i + 3)
                if s == 10:
                    dt_bias(i + 2)
                    bc_proj(i + 2)
                    sum_squares(i + 3)
                if s == 11:
                    softplus_log(i + 2)
                    roots(i + 3)
                    ln_root(i - 1)
                    bc_out(i + 2)
                if s == 12:
                    softplus(i + 2)
                    dt_tanh(i + 2)
                    ln_out(i - 1)
                    normed(i + 3)
                if s == 13:
                    dt_out(i + 2)
                    transposed(i - 1)
                if s == 15:
                    logits(i - 1)
                if s < 11:
                    decay_tanh(i + 1, 6 * s, 6 * s + 6)
                elif s > 11:
                    decay_exp(i + 1, s - 12)
                if u == 0:
                    if i >= 0:
                        z_out(q - 2)
                    if live:
                        if r == 0:
                            dt_x(q // 2)
                        mult(q, 0)
                        carry(q, 0)
                if live:
                    if u < 3:
                        mult(q, u + 1)
                        carry(q, u + 1)
                    scan(q, u)
                    squared(q, u)
                    hc(q, u)
                    if u == 3:
                        norm_sum(q)
                if u == 1:
                    if 0 <= q - 1 < 2 * NC - 2:
                        factor(q + 1)
                    y_sum(q - 1)
                if u == 3 and q + 2 >= 0:
                    bring(q + 2)

        for i in range(-4, NB + 1):
            window(i)
        for name in ("x2d", "lgd", "xe0", "bd0", "cd0", "bd1", "cd1"):
            if name in sems:
                put(SP, None, ((sems[name], sems[name].n),))
        run_block(nc, qs)


def moe_phase(nc, d, XE, X2d, LGd, YO, out):
    ctx = ExitStack()
    with ctx:
        def sb(name, shape, dt=F32):
            return ctx.enter_context(nc.sbuf_tensor(name, shape, dt))

        sems = {}

        def sem(name):
            if name not in sems:
                sems[name] = Sem(ctx.enter_context(nc.semaphore("m_" + name)))
            return sems[name]

        qs = {k: Queue() for k in ("sp", "act", "dve", "pool", "pe")}
        SP, AC, DV, PO, PE = qs["sp"], qs["act"], qs["dve"], qs["pool"], qs["pe"]
        V, S, G, M, Y = nc.vector, nc.scalar, nc.gpsimd, nc.tensor, nc.sync

        X2 = sb("X2", [128, 64, 256])
        W1 = sb("W1", [128, 2, 2, 1024])
        W2 = sb("W2", [128, 2, 8, 256])
        B1 = sb("B1", [128, 8, 8])
        B2 = sb("B2", [128, 8, 256])
        XR = sb("XRE", [128, 2, 6, 256])
        XT = sb("XTE", [128, 2, 768])
        HT = sb("HT", [128, 8, 768])
        YS = sb("YS", [128, 2, 2, 256])
        GA = sb("GA", [128, 4, 2, 256])
        ID = sb("ID2", [128, 128])
        ONE = sb("ONE2", [128, 128])
        TRI = sb("TRI", [128, 128])
        IO = sb("IO", [128, 8])
        LG = sb("LG", [128, 64, 8])
        P = sb("P", [128, 64, 8])
        VL = sb("VL", [128, 64, 8])
        OH = sb("OH", [128, 2, 64, 8])
        MM = sb("MM", [128, 64, 8])
        CN = sb("CN", [128, 8, 64])
        MK = sb("MK", [128, 8, 64])
        CI = sb("CI", [128, 8, 64])
        PO_ = sb("POS", [128, 64, 8])
        R = sb("R", [128, 16, 64])
        IX = sb("IX", [128, 4, 64], I32)
        BN = sb("BN2", [128, 4, 6])
        MV = sb("MV2", [128, 4, 2])
        SD = sb("SD2", [128, 4])
        EP = sb("EP", [128, 1])
        PB = [ctx.enter_context(nc.psum_tensor(f"PE{i}", [128, 512], F32)) for i in range(8)]

        k = {}
        lg = put(SP, lambda: Y.dma_start(ID[:], d["ident"]), (), sem("ld"), dma=True)
        lg = put(SP, lambda: Y.dma_start(TRI[:], d["tri"]), (), sem("ld"), dma=True)
        lg = put(SP, lambda: Y.dma_start(IO[:], d["iota"].to_broadcast([128, 8])), (), sem("ld"), dma=True)
        for b in range(8):
            lg = put(SP, lambda b=b: Y.dma_start(
                LG[:, 8 * b:8 * b + 8, :], LGd[b, 10:10 + L, :].rearrange("(j p) e -> p j e", p=128)),
                (), sem("ld"), dma=True)
        for b in range(8):
            k["x2", b] = put(SP, lambda b=b: Y.dma_start(
                X2[:, 8 * b:8 * b + 8, :], X2d[b, 10:10 + L, :].rearrange("(j p) n -> p j n", p=128)),
                (), sem(f"x2l{b}"), dma=True)
        put(AC, lambda: S.dma_start(B1[:], d["b1"]), (), sem("bl"), dma=True)
        bl = put(AC, lambda: S.dma_start(B2[:].rearrange("p e n -> p (e n)"),
                                         d["b2"].rearrange("e n -> (e n)").partition_broadcast(128)),
                 (), sem("bl"), dma=True)

        s = sem("rt")

        def dv(fn, *waits):
            k["c"] = put(DV, fn, (k.get("c"),) + waits, s)
            return k["c"]

        def bc(t):
            return t.unsqueeze(2).to_broadcast([128, 64, 8])

        dv(lambda: V.memset(ONE[:], 1.0))
        dv(lambda: V.memset(EP[:], 1e-5))
        dv(lambda: V.memset(MK[:], 1.0))
        dv(lambda: V.memset(MK[:, :, 0:1], 0.0))
        dv(lambda: V.tensor_reduce(R[:, 0], LG[:], AX.X, ALU.max), lg)
        t = dv(lambda: V.tensor_tensor(P[:], LG[:], bc(R[:, 0]), ALU.subtract))
        a = put(AC, lambda: S.activation(P[:], P[:], ACT.Exp), (t,), sem("ra"))
        dv(lambda: V.tensor_reduce(R[:, 1], P[:], AX.X, ALU.add), a)
        dv(lambda: V.reciprocal(R[:, 1], R[:, 1]))
        dv(lambda: V.tensor_tensor(P[:], P[:], bc(R[:, 1]), ALU.mult))
        for n in range(2):
            pk, ek = R[:, 2 + n], R[:, 4 + n]
            iob = IO[:].unsqueeze(1).to_broadcast([128, 64, 8])
            dv(lambda pk=pk: V.tensor_reduce(pk, P[:], AX.X, ALU.max))
            dv(lambda pk=pk: V.tensor_tensor(VL[:], P[:], bc(pk), ALU.is_ge))
            dv(lambda: V.scalar_tensor_tensor(VL[:], VL[:], -100.0, iob, ALU.mult, ALU.add))
            dv(lambda ek=ek: V.tensor_reduce(ek, VL[:], AX.X, ALU.min))
            dv(lambda ek=ek, n=n: V.tensor_tensor(OH[:, n], VL[:], bc(ek), ALU.is_equal))
            if n == 0:
                dv(lambda: V.scalar_tensor_tensor(P[:], OH[:, 0], -4.0, P[:], ALU.mult, ALU.add))
        t = dv(lambda: V.tensor_tensor(MM[:], OH[:, 0], OH[:, 1], ALU.add))
        put(PE, lambda: M.matmul(PB[0][:], TRI[:], MM[:].rearrange("p j e -> p (j e)"), start=True, stop=True),
            (t, lg), sem("rp"))
        t = put(PE, lambda: M.matmul(PB[1][:], ONE[:], MM[:].rearrange("p j e -> p (j e)"), start=True, stop=True),
                (), sem("rp"))
        dv(lambda: V.tensor_copy(CN[:], PB[1][:].rearrange("p (j e) -> p e j", e=8)), t)
        dv(lambda: V.tensor_tensor_scan(CI[:].rearrange("p e j -> p (e j)"), MK[:].rearrange("p e j -> p (e j)"),
                                        CN[:].rearrange("p e j -> p (e j)"), 0.0, ALU.mult, ALU.add))
        dv(lambda: V.tensor_tensor(CI[:], CI[:], CN[:], ALU.subtract))
        dv(lambda: V.tensor_tensor(PO_[:], PB[0][:].rearrange("p (j e) -> p j e", e=8),
                                   CI[:].rearrange("p e j -> p j e"), ALU.add))
        dv(lambda: V.tensor_tensor(R[:, 6], R[:, 2], R[:, 3], ALU.add))
        dv(lambda: V.reciprocal(R[:, 6], R[:, 6]))
        for n in range(2):
            dv(lambda n=n: V.tensor_tensor(VL[:], PO_[:], OH[:, n], ALU.mult))
            dv(lambda: V.tensor_reduce(R[:, 7], VL[:], AX.X, ALU.add))
            dv(lambda n=n: V.tensor_scalar(R[:, 8 + n], R[:, 7], float(CAP), None, ALU.is_lt))
            dv(lambda n=n: V.tensor_scalar(R[:, 10], R[:, 4 + n], 100.0, float(CAP), ALU.add, ALU.mult))
            dv(lambda n=n: V.tensor_scalar(R[:, 11], R[:, 8 + n], -100000.0, 100000.0, ALU.mult, ALU.add))
            dv(lambda: V.tensor_tensor(R[:, 11], R[:, 11], R[:, 7], ALU.add))
            dv(lambda: V.tensor_tensor(R[:, 11], R[:, 11], R[:, 10], ALU.add))
            k["sc"] = dv(lambda n=n: V.tensor_copy(IX[:, n], R[:, 11]))
            dv(lambda n=n: V.tensor_tensor(R[:, 7], R[:, 7], R[:, 8 + n], ALU.mult))
            dv(lambda: V.tensor_tensor(R[:, 7], R[:, 7], R[:, 10], ALU.add))
            dv(lambda n=n: V.tensor_copy(IX[:, 2 + n], R[:, 7]))
            dv(lambda n=n: V.tensor_tensor(R[:, 12 + n], R[:, 2 + n], R[:, 6], ALU.mult))
            k["g"] = dv(lambda n=n: V.tensor_tensor(R[:, 12 + n], R[:, 12 + n], R[:, 8 + n], ALU.mult))

        for j in range(64):
            for n in range(2):
                k["disp"] = put(PO, lambda j=j, n=n: G.indirect_dma_start(
                    out=XE, out_offset=bass.IndirectOffsetOnAxis(ap=IX[:, n, j:j + 1].bitcast(U32), axis=0),
                    in_=X2[:, j, :], in_offset=None, bounds_check=E * CAP - 1, oob_is_err=False),
                    (k["g"], k["x2", j // 8]), sem("disp"), dma=True)

        def load_w(e):
            if e < E:
                put(AC, lambda: S.dma_start(W1[:, e % 2], d["w1"][e].rearrange("(a p) n -> p a n", p=128)),
                    (k.get(("h", e - 2)),), sem(f"wl{e % 2}"), dma=True)
                k["w", e] = put(AC, lambda: S.dma_start(W2[:, e % 2], d["w2"][e].rearrange("(a p) n -> p a n", p=128)),
                                (k.get(("y", e - 2)),), sem(f"wl{e % 2}"), dma=True)

        def load_e(e):
            if e < E:
                k["xe", e] = put(SP, lambda: Y.dma_start(
                    XR[:, e % 2], XE[e * CAP:(e + 1) * CAP, :].rearrange("(s p) n -> p s n", p=128)),
                    (k["disp"], k.get(("xt", e - 2))), sem(f"xe{e % 2}"), dma=True)

        free = {}
        nb = [2]

        def bank():
            n = nb[0] % 8
            nb[0] += 1
            return n, PB[n], [free.get(n)]

        load_w(0)
        load_w(1)
        load_e(0)
        load_e(1)
        for e in range(E):
            for c in range(3):
                n, p, waits = bank()
                for a in range(2):
                    for h in range(2):
                        o = p[:, 256 * a + 128 * h:256 * a + 128 * h + 128]
                        t = put(PE, lambda o=o, a=a, h=h, c=c, e=e: M.transpose(
                            o, XR[:, e % 2, 2 * c + h, 128 * a:128 * a + 128], ID[:]),
                            waits + [k["xe", e], lg, k["g"]], sem("xt"))
                free[n] = put(DV, lambda p=p, c=c: V.tensor_copy(
                    XT[:, :, 256 * c:256 * c + 256], p[:].rearrange("p (a n) -> p a n", a=2)),
                    (t, k.get(("h", e - 1))), sem("xtc"))
            k["xt", e] = t
            xc = free[n]
            load_e(e + 2)
            for m in range(8):
                for h in range(2):
                    n, p, waits = bank()
                    for a in range(2):
                        t = put(PE, lambda p=p, a=a, m=m, h=h, e=e: M.matmul(
                            p[:, 0:384], W1[:, e % 2, a, 128 * m:128 * m + 128], XT[:, a, 384 * h:384 * h + 384],
                            start=a == 0, stop=a == 1), waits + [xc, k["w", e]], sem("h"))
                    if h == 0:
                        free[n] = r0 = put(AC, lambda p=p, m=m, h=h, e=e: S.activation(
                            HT[:, m, 384 * h:384 * h + 384], p[:, 0:384], ACT.Relu, bias=B1[:, e, m:m + 1]),
                            (t, bl, k.get(("y", e - 1))), sem("ra"))
                    else:
                        free[n] = r1 = put(DV, lambda p=p, m=m, h=h, e=e: V.tensor_scalar(
                            HT[:, m, 384 * h:384 * h + 384], p[:, 0:384], B1[:, e, m:m + 1], 0.0,
                            ALU.add, ALU.max), (t, bl, k.get(("y", e - 1))), sem("rv"))
            k["h", e] = t
            for c in range(3):
                n, p, waits = bank()
                for h in range(2):
                    for m in range(8):
                        t = put(PE, lambda p=p, m=m, h=h, c=c, e=e: M.matmul(
                            p[:, 256 * h:256 * h + 256], HT[:, m, 128 * (2 * c + h):128 * (2 * c + h) + 128],
                            W2[:, e % 2, m, :], start=m == 0, stop=m == 7), waits + [r0, r1], sem("y"))
                i = 3 * e + c
                free[n] = t2 = put(DV, lambda p=p, i=i, e=e: V.tensor_tensor(
                    YS[:, i % 2], p[:].rearrange("p (h n) -> p h n", h=2),
                    B2[:, e].unsqueeze(1).to_broadcast([128, 2, 256]), ALU.add),
                    (t, k.get(("yo", i - 2))), sem("ys"))
                k["yo", i] = put(SP, lambda i=i: Y.dma_start(
                    YO[256 * i:256 * i + 256, :].rearrange("(h p) n -> p h n", p=128), YS[:, i % 2]),
                    (t2,), sem(f"yo{i % 2}"), dma=True)
            k["y", e] = t
            load_w(e + 2)

        yo = (k["yo", 22], k["yo", 23])

        def gather(j):
            for n in range(2):
                k["ga", j] = put(PO, lambda n=n: G.indirect_dma_start(
                    out=GA[:, j % 4, n], out_offset=None, in_=YO,
                    in_offset=bass.IndirectOffsetOnAxis(ap=IX[:, 2 + n, j:j + 1].bitcast(U32), axis=0),
                    bounds_check=E * CAP - 1, oob_is_err=False), yo + (k.get(("a", j - 4)),),
                    sem(f"ga{j % 4}"), dma=True)

        def combine(j):
            t = put(DV, lambda: V.scalar_tensor_tensor(
                X2[:, j], GA[:, j % 4, 0], R[:, 12, j:j + 1], X2[:, j], ALU.mult, ALU.add),
                (k["ga", j], k["disp"]), sem("ca"))
            k["a", j] = t = put(DV, lambda: V.scalar_tensor_tensor(
                X2[:, j], GA[:, j % 4, 1], R[:, 13, j:j + 1], X2[:, j], ALU.mult, ALU.add), (t,), sem("ca"))
            t = put(DV, lambda: V.bn_stats(BN[:, j % 4], X2[:, j]), (t, k.get(("mv", j - 4))), sem("ca"))
            k["mv", j] = put(DV, lambda: V.bn_aggr(MV[:, j % 4], BN[:, j % 4]), (t, k.get(("x3", j - 4))), sem("ca"))
            k["sd", j] = put(AC, lambda: S.activation(SD[:, j % 4:j % 4 + 1], MV[:, j % 4, 1:2], ACT.Sqrt,
                                                      bias=EP[:]), (k["mv", j],), sem("sd"))

        def finish(j):
            t = put(DV, lambda: V.reciprocal(SD[:, j % 4:j % 4 + 1], SD[:, j % 4:j % 4 + 1]), (k["sd", j],), sem("ca"))
            k["x3", j] = put(DV, lambda: V.tensor_scalar(X2[:, j], X2[:, j], MV[:, j % 4, 0:1],
                                                         SD[:, j % 4:j % 4 + 1], ALU.subtract, ALU.mult),
                             (t,), sem("ca"))
            k["out"] = put(SP, lambda: Y.dma_start(out[128 * j:128 * j + 128, :], X2[:, j]), (k["x3", j],),
                           sem("out"), dma=True)

        for j in range(64 + 1):
            if j < 64:
                gather(j)
                combine(j)
            if j >= 1:
                finish(j - 1)
        put(SP, None, (k["out"],))
        run_block(nc, qs)


def build(nc, d, out):
    XE = nc.dram_tensor("XE", [E * CAP, DM], F32, kind="Internal").ap()
    YO = nc.dram_tensor("YO", [E * CAP, DM], F32, kind="Internal").ap()
    X2d = nc.dram_tensor("X2d", [B, LP, DM], F32, kind="Internal").ap()
    LGd = nc.dram_tensor("LGd", [B, LP, E], F32, kind="Internal").ap()
    Bd = nc.dram_tensor("Bd", [NC, 2, NS, 40], F32, kind="Internal").ap()
    Cd = nc.dram_tensor("Cd", [NC, 2, NS, 40], F32, kind="Internal").ap()
    ssm_phase(nc, d, XE, X2d, LGd, Bd, Cd)
    moe_phase(nc, d, XE, X2d, LGd, YO, out)


def kernel(**inputs):
    import concourse.bacc as bacc
    from concourse.bass_utils import run_bass_kernel_spmd

    a = {n: np.asarray(v) for n, v in inputs.items()}
    x = a["L0_attn_x"]
    xp = np.zeros((B, LP + 1, DM), np.float32)
    xp[:, 10:10 + L] = x
    xT = xp[:, 1:].reshape(B, NB, T, 2, 128).transpose(1, 4, 3, 0, 2).reshape(NB, 128, 2, B * T)
    wbc = np.zeros((DI, 64), np.float32)
    wbc[:, 0:16] = a["L0_attn_W_B"].T
    wbc[:, 32:48] = a["L0_attn_W_C"].T
    arrays = {
        "xT": xT, "xp": xp[:, :LP],
        "w_in": a["L0_attn_W_in"].T, "w_dt": a["L0_attn_W_dt"].T, "w_bc": wbc, "w_out": a["L0_attn_W_out"].T,
        "a_log": a["L0_attn_A_log"], "conv_w": a["L0_attn_conv_w"].reshape(DI, 4), 
        "vecs": np.stack([a[n].reshape(4, 128).T for n in ("L0_attn_conv_b", "L0_attn_b_dt", "L0_attn_D_param")], 1),
        "norm_w": a["L0_attn_norm_w"].reshape(2, 128).T,
        "res": a["L0_attn_residual_scale"].reshape(1, 1), "w_router": a["L0_ffn_w_router"],
        "w1": a["L0_ffn_w1"], "b1": a["L0_ffn_b1"].reshape(E, 8, 128).transpose(2, 0, 1), "w2": a["L0_ffn_w2"], "b2": a["L0_ffn_b2"],
        "ident": np.eye(128, dtype=np.float32), "tri": np.triu(np.ones((128, 128), np.float32), 1),
        "iota": np.arange(8, dtype=np.float32).reshape(1, 8),
    }
    nc = bacc.Bacc("TRN2", target_bir_lowering=False, num_devices=1)
    feed, d = {}, {}
    for n, v in arrays.items():
        v = np.ascontiguousarray(v)
        feed[f"in_{n}"] = v
        d[n] = nc.dram_tensor(f"in_{n}", v.shape, mybir.dt.from_np(v.dtype), kind="ExternalInput").ap()
    out = nc.dram_tensor("out_y", [B * L, DM], F32, kind="ExternalOutput").ap()
    build(nc, d, out)
    r = run_bass_kernel_spmd(nc, [feed], core_ids=[0])
    return r.results[0]["out_y"].reshape(B, L, DM)
```

```python
import numpy as np
import concourse.bass as bass
from concourse import mybir
from contextlib import ExitStack

F32 = mybir.dt.float32
I32 = mybir.dt.int32
U32 = mybir.dt.uint32
ALU = mybir.AluOpType
ACT = mybir.ActivationFunctionType
AX = mybir.AxisListType

B, L, DM, DI, NS = 8, 1024, 256, 512, 16
E, HF, CAP = 8, 1024, 768
T = 20
NB = 52
LP = NB * T
NC = 2 * NB
CH = 704


class Queue:

    def __init__(self):
        self.items = []
        self.side = None

    def play(self, eng):
        seen = {}
        for waits, fn, sem, inc in self.items:
            for s, v in waits:
                if seen.get(s, 0) < v:
                    eng.wait_ge(s.h, v)
                    seen[s] = v
            if fn is None:
                continue
            ins = fn()
            if sem is not None:
                ins.then_inc(sem.h, inc)


class Sem:

    def __init__(self, h):
        self.h, self.n = h, 0


def put(q, fn, waits=(), sem=None, dma=False):
    inc = 16 if dma else 1
    tok = None
    if sem is not None:
        sem.n += inc
        tok = (sem, sem.n)
    q.items.append(([w for w in waits if w is not None], fn, sem, inc))
    if q.side is not None:
        side, q.side = q.side, None
        if next(side, True) is None:
            q.side = side
    return tok


def rest(q):
    side, q.side = q.side, None
    for _ in side or ():
        pass


def run_block(nc, qs):
    with nc.Block() as block:
        @block.sync
        def _(eng):
            qs["sp"].play(eng)

        @block.scalar
        def _(eng):
            qs["act"].play(eng)

        @block.vector
        def _(eng):
            qs["dve"].play(eng)

        @block.gpsimd
        def _(eng):
            qs["pool"].play(eng)

        @block.tensor
        def _(eng):
            qs["pe"].play(eng)


def ssm_phase(nc, d, XE, X2d, LGd, Bd, Cd):
    ctx = ExitStack()
    with ctx:
        def sb(name, shape, dt=F32):
            return ctx.enter_context(nc.sbuf_tensor(name, shape, dt))

        sems = {}

        def sem(name):
            if name not in sems:
                sems[name] = Sem(ctx.enter_context(nc.semaphore(name)))
            return sems[name]

        qs = {k: Queue() for k in ("sp", "act", "dve", "pool", "pe")}
        SP, AC, DV, PO, PE = qs["sp"], qs["act"], qs["dve"], qs["pool"], qs["pe"]
        V, S, G, M, Y = nc.vector, nc.scalar, nc.gpsimd, nc.tensor, nc.sync

        DA = sb("DA", [128, 4, 8, 4, 16, 11])
        H = sb("H", [128, 3, 4, CH])
        BB = sb("BB", [128, 3, 16, 4, 10])
        CB = sb("CB", [128, 3, 16, 4, 10])
        WIN = sb("WIN", [128, 2, 1024])
        WDT = sb("WDT", [128, 4, 512])
        WBC = sb("WBC", [128, 4, 64])
        WO = sb("WO", [128, 4, 256])
        WR = sb("WR", [128, 2, 8])
        ID = sb("ID", [128, 128])
        ONE = sb("ONE", [128, 128])
        MEAN = sb("MEAN", [128, 128])
        AS = sb("AS", [128, 4, 16])
        CW = sb("CW", [128, 4, 4])
        PV = sb("PV", [128, 3, 4])
        NW = sb("NW", [128, 2])
        SC = sb("SC", [128, 2])
        CST = sb("CST", [128, 4])
        XT = sb("XT", [128, 2, 2, 160])
        XN = sb("XN", [128, 2, 2, 160])
        RST = sb("RST", [128, 160])
        XB = sb("XB", [128, 4, 8, 23])
        TA = sb("TA", [128, 4, 8, 20])
        TB = sb("TB", [128, 4, 8, 20])
        TC = sb("TC", [128, 4, 8, 20])
        XC = sb("XC", [128, 2, 4, 8, 20])
        DT = sb("DT", [128, 2, 4, 8, 20])
        SG = sb("SG", [128, 2, 4, 8, 21])
        DX = sb("DX", [128, 2, 4, 8, 21])
        Z = sb("Z", [128, 4, 8, 20])
        BS = sb("BS", [16, 2, 8, 10])
        CS = sb("CS", [64, 4, 8, 10])
        XR = sb("XR", [80, 2, 256])
        VV = sb("VV", [80, 2, 256])
        BN = sb("BN", [80, 2, 6])
        MVR = sb("MVR", [80, 2, 2])
        SD = sb("SD", [80, 2])
        X2T = sb("X2T", [128, 4, 80])
        LGS = sb("LGS", [80, 2, 8])
        SS = sb("SS", [128, 2, 4])
        JK = sb("JK", [128, 2, 64])
        FW = sb("FW", [128, 2, 4, 4])
        FI = sb("FI", [128, 2, 4], I32)
        FC = sb("FC", [128, 2, 4])
        PM = ctx.enter_context(nc.psum_tensor("PM", [128, 2048], F32))
        PB = [ctx.enter_context(nc.psum_tensor(f"PB{i}", [128, 512], F32)) for i in range(2)]

        YB = [ctx.enter_context(nc.psum_tensor(f"YB{i}", [128, 512], F32)) for i in range(2)]

        def U(c):
            return PM[:, 320 * (c % 2):320 * (c % 2) + 320].rearrange("p (a b t) -> p a b t", a=4, b=8)

        def DBX(u):
            return PM[:, 640 + CH * (u % 2):640 + CH * (u % 2) + CH]

        def YP(q):
            return YB[q % 2][:, 0:160]

        def NP(g):
            return YB[g][:, 256:260]

        w = []
        for k, (dst, src) in enumerate([
                (WIN[:], d["w_in"].rearrange("(a p) n -> p a n", p=128)),
                (WDT[:], d["w_dt"].rearrange("(a p) n -> p a n", p=128)),
                (WBC[:], d["w_bc"].rearrange("(a p) n -> p a n", p=128)),
                (WO[:], d["w_out"].rearrange("(a p) n -> p a n", p=128)),
                (WR[:], d["w_router"].rearrange("(a p) n -> p a n", p=128)),
                (ID[:], d["ident"]),
                (AS[:], d["a_log"].rearrange("(a p) n -> p a n", p=128)),
                (CW[:], d["conv_w"].rearrange("(a p) n -> p a n", p=128)),
                (PV[:], d["vecs"]),
                (NW[:], d["norm_w"]),
                (SC[:, 0:1], d["res"].to_broadcast([128, 1])),
        ]):
            w.append(put(AC, lambda dst=dst, src=src: S.dma_start(dst, src), (), sem("w_load"), dma=True))
        wall = w[-1]
        s_pre = sem("pre")
        c1 = put(DV, lambda: V.memset(ONE[:], 1.0), (), s_pre)
        c1 = put(DV, lambda: V.memset(MEAN[:], 1.0 / 256), (), s_pre)
        KD = 0.5 / (0.0495 + 1e-8)
        for col, val in enumerate((1e-6, 1e-5, -0.0505 * KD, 0.0)):
            c1 = put(DV, lambda col=col, val=val: V.memset(CST[:, col:col + 1], val), (), s_pre)
        c1 = put(DV, lambda: V.memset(XB[:], 0.0), (), s_pre)
        c1 = put(DV, lambda: V.memset(CS[:], 0.0), (), s_pre)
        c1 = put(DV, lambda: V.memset(SG[:], 0.0), (), s_pre)
        c1 = put(DV, lambda: V.memset(DX[:], 0.0), (), s_pre)
        c1 = put(DV, lambda: V.memset(DA[:, :, :, :, :, 0:1].rearrange("p c b a n t -> p (c b a n) t"), 0.0), (), s_pre)
        z0 = put(PO, lambda: G.memset(H[:], 0.0), (), sem("h0"))
        ze = None
        ROWS = H[:].rearrange("p a b c -> p (a b c)")
        for k in range(2):
            dst = XE[k * 3072:(k + 1) * 3072, :].rearrange("(p r) n -> p (r n)", p=128)
            ze = put(SP, lambda dst=dst: Y.dma_start(dst, ROWS[:, 0:6144]), (z0,), sem("xe0"), dma=True)
        c1 = put(DV, lambda: V.tensor_scalar(CW[:], CW[:], 0.5, None, ALU.mult), (wall,), s_pre)
        c1 = put(DV, lambda: V.tensor_scalar(PV[:, 0, :], PV[:, 0, :], 0.5, None, ALU.mult), (), s_pre)
        a1 = put(AC, lambda: S.activation(AS[:], AS[:], ACT.Tanh, scale=0.5 / (5.0 + 1e-8)), (wall,), sem("pre_a"))
        a1 = put(AC, lambda: S.activation(AS[:], AS[:], ACT.Exp, scale=10.0), (a1,), sem("pre_a"))
        c1 = put(DV, lambda: V.tensor_scalar(AS[:], AS[:], -0.5 / (8.0 + 1e-8), None, ALU.mult), (a1,), s_pre)
        a1 = put(AC, lambda: S.activation(SC[:, 1:2], SC[:, 0:1], ACT.Tanh, scale=0.5), (), sem("pre_a"))
        c1 = put(DV, lambda: V.tensor_scalar(SC[:, 0:1], SC[:, 1:2], 0.125, 0.125, ALU.mult, ALU.add), (a1,), s_pre)
        pre = put(DV, lambda: V.tensor_scalar(WO[:], WO[:], SC[:, 0:1], None, ALU.mult), (c1,), s_pre)

        k = {}
        bank_free = [[None], [None]]
        nbank = [0]

        def bank():
            n = nbank[0] % 2
            nbank[0] += 1
            assert bank_free[n]
            waits, bank_free[n] = bank_free[n], []
            return n, PB[n], waits

        def mms(specs, waits, s):
            tok = None
            for n, (o, l, r, st, sp) in enumerate(specs):
                tok = put(PE, lambda o=o, l=l, r=r, st=st, sp=sp: M.matmul(o, l, r, start=st, stop=sp),
                          waits if n == 0 else (), s if n == len(specs) - 1 else None)
            return tok

        def ok(j):
            return 0 <= j < NB

        def load_x(j):
            if ok(j):
                k["xt", j] = put(SP, lambda: Y.dma_start(XT[:, j % 2], d["xT"][j]),
                                 (k.get(("xn", j - 2)), k.get(("sq", j - 2))), sem(f"xt{j % 2}"), dma=True)

        def squares(j):
            if ok(j):
                k["sq", j] = put(AC, lambda: S.activation(XN[:, j % 2], XT[:, j % 2], ACT.Square),
                                 (k["xt", j], k.get(("gate", j - 2))), sem("sq"))

        def sum_squares(j):
            if ok(j):
                n, p, waits = bank()
                sq = XN[:, j % 2]
                k["ssum", j] = mms([(p[:, 0:160], MEAN[:], sq[:, 0], True, False),
                                    (p[:, 0:160], MEAN[:], sq[:, 1], False, True)],
                                   [k["sq", j], pre] + waits, sem("ssum"))
                k["rt", j] = (n, p)

        def roots(j):
            if ok(j):
                n, p = k["rt", j]
                k["root", j] = put(AC, lambda: S.activation(RST[:], p[:, 0:160], ACT.Ln, bias=CST[:, 0:1]),
                                   (k["ssum", j], k.get(("xn", j - 1)), pre), sem("root"))
                bank_free[n].append(k["root", j])

        def inv_roots(j):
            if ok(j):
                k["rs", j] = put(AC, lambda: S.activation(RST[:], RST[:], ACT.Exp, scale=-0.5),
                                 (k["root", j],), sem("rs"))

        def normed(j):
            if ok(j):
                for a in range(2):
                    k["xn", j] = put(DV, lambda a=a: V.scalar_tensor_tensor(
                        XN[:, j % 2, a], XT[:, j % 2, a], NW[:, a:a + 1], RST[:], ALU.mult, ALU.mult),
                        (k["rs", j],), sem("xn"))

        def halo(j):
            if ok(j) and j > 0:
                k["halo", j] = put(PO, lambda: G.tensor_copy(XB[:, :, :, 0:3], XB[:, :, :, 20:23]),
                                   (k["conv", j - 1],), sem("halo"))

        def project(j, first, name):
            if not ok(j):
                return
            out = []
            for m in range(2):
                n, p, waits = bank()
                sp = []
                for a in range(2):
                    c = first + 256 * m + 128 * a
                    for kk in range(2):
                        sp.append((p[:, 160 * a:160 * a + 160], WIN[:, kk, c:c + 128], XN[:, j % 2, kk],
                                   kk == 0, kk == 1))
                tok = mms(sp, [k["xn", j]] + waits, sem("proj"))
                out.append((n, p, tok))
            k[name, j] = tok
            k[name + "_b", j] = out

        def branch_out(j):
            if ok(j):
                for m, (n, p, tok) in enumerate(k["br_b", j]):
                    k["xb", j] = put(AC, lambda m=m, p=p: S.activation(
                        XB[:, 2 * m:2 * m + 2, :, 3:23], p[:, 0:320].rearrange("p (a b t) -> p a b t", a=2, b=8),
                        ACT.Copy), (tok, k.get(("halo", j)), k.get(("conv", j - 1)), pre), sem("xb"))
                    bank_free[n].append(k["xb", j])

        def conv(j, part):
            if not ok(j):
                return
            sc = sem("conv")
            if part == 0:
                for a in range(4):
                    k["cv", j] = put(PO, lambda a=a: G.tensor_scalar(
                        TA[:, a], XB[:, a, :, 0:20], CW[:, a, 0:1], PV[:, 0, a:a + 1], ALU.mult, ALU.add),
                        (k["xb", j], k.get(("halo", j)), k.get(("dt", j - 1)), pre), sc)
            if part > 0:
                k["conv", j] = k["cv", j] = put(PO, lambda: G.tensor_tensor(TA[:], TA[:], TC[:], ALU.add),
                                                (k["ct", j],), sc)
            if part < 3:
                tap = part + 1
                wv = CW[:, :, tap:tap + 1].unsqueeze(3).to_broadcast([128, 4, 8, 20])
                k["ct", j] = put(PO, lambda: G.tensor_tensor(TC[:], XB[:, :, :, tap:tap + 20], wv, ALU.mult),
                                 (k["cv", j], k.get(("dx", j - 2))), sc)

        def silu_tanh(j):
            if ok(j):
                k["th", j] = put(AC, lambda: S.activation(TB[:], TA[:], ACT.Tanh),
                                 (k["conv", j], k.get(("sg", j - 1))), sem("th"))

        def silu(j):
            if ok(j):
                k["xc", j] = put(DV, lambda: V.scalar_tensor_tensor(
                    XC[:, j % 2].rearrange("p a b t -> p (a b t)"), TB[:].rearrange("p a b t -> p (a b t)"), 1.0,
                    TA[:].rearrange("p a b t -> p (a b t)"), ALU.add, ALU.mult),
                    (k["th", j], k.get(("bc", j - 2)), k.get(("dx", j - 2)), k.get(("u", 2 * j - 3))), sem("xc"))

        def dt_proj(j):
            if not ok(j):
                return
            out = []
            for m in range(2):
                n, p, waits = bank()
                sp = []
                for a in range(2):
                    c = 256 * m + 128 * a
                    for kk in range(4):
                        sp.append((p[:, 160 * a:160 * a + 160], WDT[:, kk, c:c + 128],
                                   XC[:, j % 2, kk].rearrange("p b t -> p (b t)"), kk == 0, kk == 3))
                out.append((n, p, mms(sp, [k["xc", j]] + waits, sem("dtp"))))
            k["dtp", j] = out

        def bc_proj(j):
            if not ok(j):
                return
            n, p, waits = bank()
            k["bc", j] = mms([(p[0:64, 0:160], WBC[:, kk, :], XC[:, j % 2, kk].rearrange("p b t -> p (b t)"),
                               kk == 0, kk == 3) for kk in range(4)], waits, sem("bcp"))
            k["bcb", j] = (n, p)

        def dt_bias(j):
            if not ok(j):
                return
            for m, (n, p, tok) in enumerate(k["dtp", j]):
                for a in range(2):
                    k["dtb", j] = put(AC, lambda m=m, a=a, p=p: S.activation(
                        TA[:, 2 * m + a].rearrange("p b t -> p (b t)"), p[:, 160 * a:160 * a + 160],
                        ACT.Identity, bias=PV[:, 1, 2 * m + a:2 * m + a + 1]), (tok,), sem("dtb"))
                bank_free[n].append(k["dtb", j])

        def bc_out(j):
            if not ok(j):
                return
            n, p = k["bcb", j]
            pv = p[:, 0:160].rearrange("p (b c t) -> p c b t", b=8, c=2)
            b = put(AC, lambda: S.activation(BS[:], pv[0:16], ACT.Copy),
                    (k["bc", j], k.get(("bd", j - 1))), sem("bcs"))
            q0 = (2 * j) % 4
            put(AC, lambda: S.activation(CS[32:48, q0:q0 + 2, :, 1:10], pv[32:48, :, :, 0:9], ACT.Copy),
                (k.get(("cd", j - 2)), pre), sem("bcs"))
            put(AC, lambda: S.activation(CS[32:48, q0 + 1, :, 0:1], pv[32:48, 0, :, 9:10], ACT.Copy),
                (), sem("bcs"))
            c = put(AC, lambda: S.activation(CS[32:48, (q0 + 2) % 4, :, 0:1], pv[32:48, 1, :, 9:10], ACT.Copy),
                    (k.get(("cd", j - 1)),), sem("bcs"))
            bank_free[n].append(c)
            for gg in range(2):
                k["bd", j] = put(SP, lambda gg=gg: Y.dma_start(
                    Bd[2 * j:2 * j + 2, gg].rearrange("c n e -> n c e"),
                    BS[:, :, 4 * gg:4 * gg + 4, :].rearrange("n c b t -> n c (b t)")), (b,), sem(f"bd{j % 2}"), dma=True)
                k["cd", j] = put(SP, lambda gg=gg: Y.dma_start(
                    Cd[2 * j:2 * j + 2, gg].rearrange("c n e -> n c e"),
                    CS[32:48, q0:q0 + 2, 4 * gg:4 * gg + 4, :].rearrange("n c b t -> n c (b t)")),
                    (c,), sem(f"cd{j % 2}"), dma=True)

        def softplus_log(j):
            if not ok(j):
                return
            t = put(AC, lambda: S.activation(TB[:], TA[:], ACT.Abs),
                    (k["dtb", j], k["xc", j]), sem("sp"))
            t = put(AC, lambda: S.activation(TB[:], TB[:], ACT.Exp, scale=-1.0), (t,), sem("sp"))
            k["ln", j] = put(AC, lambda: S.activation(TB[:], TB[:], ACT.Ln, bias=ONE[:, 0:1]), (t,), sem("sp"))

        def softplus(j):
            if ok(j):
                k["spl", j] = put(DV, lambda: V.scalar_tensor_tensor(
                    TA[:].rearrange("p a b t -> p (a b t)"), TA[:].rearrange("p a b t -> p (a b t)"), 0.0,
                    TB[:].rearrange("p a b t -> p (a b t)"), ALU.max, ALU.add), (k["ln", j],), sem("spl"))

        def dt_tanh(j):
            if ok(j):
                k["dth", j] = put(AC, lambda: S.activation(TA[:], TA[:], ACT.Tanh, bias=CST[:, 2:3], scale=KD),
                                  (k["spl", j],), sem("dth"))

        def dt_out(j):
            if ok(j):
                k["dt", j] = put(DV, lambda: V.tensor_scalar(DT[:, j % 2], TA[:], 0.0495 / 0.5, 0.0505, ALU.mult, ALU.add),
                                 (k["dth", j], k.get(("z64", j - 2)), k.get(("u", 2 * j - 3))), sem("dt"))

        def dt_x(c):
            j, cc = c // 2, c % 2
            t = slice(10 * cc, 10 * cc + 10)
            k["u", c] = put(DV, lambda: V.tensor_tensor(U(c), DT[:, j % 2, :, :, t], XC[:, j % 2, :, :, t], ALU.mult),
                            (k["dt", j], k["xc", j], k.get(("m1", 2 * (c - 2) + 1))), sem("u"))
            if c == 0:
                k["u", c] = put(DV, lambda: V.memset(U(0).rearrange("p a b t -> p (a b) t")[:, :, 0:9], 0.0),
                                (k["u", c],), sem("u"))

        def gate_tanh(j):
            if ok(j):
                for m, (n, p, tok) in enumerate(k["gate_b", j]):
                    k["tg", j] = put(AC, lambda m=m, p=p: S.activation(
                        TB[:, 2 * m:2 * m + 2].rearrange("p a b t -> p (a b t)"), p[:, 0:320], ACT.Tanh, scale=0.5),
                        (tok, k.get(("spl", j))), sem("tg"))

        def gate(j):
            if not ok(j):
                return
            if j > 0:
                k["sgh", j] = put(PO, lambda: G.tensor_copy(SG[:, j % 2, :, :, 0:1], SG[:, 1 - j % 2, :, :, 20:21]),
                                  (k["sg", j - 1], k.get(("z", 4 * j - 5))), sem("sgh"))
            for m, (n, p, tok) in enumerate(k["gate_b", j]):
                for a in range(2):
                    k["sg", j] = put(DV, lambda m=m, a=a, p=p: V.scalar_tensor_tensor(
                        SG[:, j % 2, 2 * m + a, :, 1:21], TB[:, 2 * m + a], 1.0,
                        p[:, 160 * a:160 * a + 160].rearrange("p (b t) -> p b t", b=8), ALU.add, ALU.mult),
                        (k["tg", j], k.get(("z", 4 * j - 5)), k.get(("dx", j - 2))), sem("sg"))
                bank_free[n].append(k["sg", j])

        def gate_d(j):
            if not ok(j):
                return
            if j > 0:
                put(PO, lambda: G.tensor_copy(DX[:, j % 2, :, :, 0:1], DX[:, 1 - j % 2, :, :, 20:21]),
                    (k["dx", j - 1], k.get(("z", 4 * j - 5))), sem("dx"))
            dv = PV[:, 2, :].unsqueeze(2).unsqueeze(3).to_broadcast([128, 4, 8, 20])
            k["xd", j] = put(PO, lambda: G.tensor_tensor(TC[:], XC[:, j % 2], dv, ALU.mult),
                             (k["xc", j], k.get(("conv", j + 1))), sem("xd"))
            k["dx", j] = put(PO, lambda: G.tensor_tensor(DX[:, j % 2, :, :, 1:21], TC[:], SG[:, j % 2, :, :, 1:21],
                                                         ALU.mult), (k["xd", j], k["sg", j]), sem("dx"))

        def decay_tanh(j, n0, n1):
            if not ok(j):
                return
            for n in range(n0, min(n1, 64)):
                a, s = n // 16, n % 16
                c0 = (2 * j) % 4
                k["z64", j] = put(AC, lambda a=a, s=s: S.activation(
                    DA[:, c0:c0 + 2, :, a, s, 1:11].rearrange("p c b t -> p b c t"),
                    DT[:, j % 2, a].rearrange("p b (c t) -> p b c t", c=2), ACT.Tanh, scale=AS[:, a, s:s + 1]),
                    (k["dt", j], k.get(("scan", 4 * (j - 2) + 3)), pre), sem("z64"))

        def decay_exp(j, r):
            if ok(j):
                c, g = r // 2, r % 2
                v = DA[:, (2 * j + c) % 4, 4 * g:4 * g + 4].rearrange("p b a n t -> p (b a n) t")[:, :, 1:11]
                k["da", 4 * j + r] = put(AC, lambda: S.activation(v, v, ACT.Exp, scale=16.0),
                                         (k["z64", j],), sem("da"))

        def bring(q):
            if 0 <= q < 2 * NC:
                c, g = q // 2, q % 2
                j = c // 2
                k["bb", q] = put(SP, lambda: Y.dma_start(
                    BB[:, q % 3].rearrange("p n b t -> p (n b t)"),
                    Bd[c, g].rearrange("n e -> (n e)").partition_broadcast(128)),
                    (k["bd", j], k.get(("m1", q - 3))), sem(f"bb{q % 3}"), dma=True)
                k["cb", q] = put(SP, lambda: Y.dma_start(
                    CB[:, q % 3].rearrange("p n b t -> p (n b t)"),
                    Cd[c, g].rearrange("n e -> (n e)").partition_broadcast(128)),
                    (k["cd", j], k.get(("hc", q - 3))), sem(f"cb{q % 3}"), dma=True)

        def factor(q):
            g = q % 2
            s = sem("fac")
            sq, y, n, w = FW[:, g, 0], FW[:, g, 1], FW[:, g, 2], FW[:, g, 3]
            t = put(DV, lambda: V.tensor_scalar(sq, NP(g), 1e-30, None, ALU.max),
                    (k["nrm", q - 2], k.get(("ca", q - 2))), s)
            k["nread", q - 2] = t
            yield
            t = put(DV, lambda: V.tensor_scalar(FI[:, g], sq.bitcast(I32), 1, None, ALU.logical_shift_right),
                    (t,), s)
            yield
            t = put(DV, lambda: V.tensor_scalar(y.bitcast(I32), FI[:, g], -1, 0x5f3759df, ALU.mult, ALU.add),
                    (t,), s)
            yield
            t = put(DV, lambda: V.tensor_tensor(n, sq, y, ALU.mult), (t,), s)
            yield
            t = put(DV, lambda: V.tensor_tensor(w, n, y, ALU.mult), (t,), s)
            yield
            t = put(DV, lambda: V.scalar_tensor_tensor(w, w, -10.0 / 3, w, ALU.add, ALU.mult), (t,), s)
            yield
            t = put(DV, lambda: V.scalar_tensor_tensor(y, w, 5.0, y, ALU.add, ALU.mult), (t,), s)
            yield
            t = put(DV, lambda: V.tensor_tensor(n, sq, y, ALU.mult), (t,), s)
            yield
            t = put(DV, lambda: V.tensor_tensor(w, n, y, ALU.mult), (t,), s)
            yield
            t = put(DV, lambda: V.scalar_tensor_tensor(n, w, -64.0 / 3, n, ALU.add, ALU.mult), (t,), s)
            yield
            t = put(DV, lambda: V.tensor_scalar(n, n, -27.0 / 1024, 1e-8, ALU.mult, ALU.add), (t,), s)
            yield
            t = put(DV, lambda: V.reciprocal(n, n), (t,), s)
            yield
            k["fac", q] = put(DV, lambda: V.tensor_scalar(FC[:, g], n, 20.0, 1.0, ALU.mult, ALU.min), (t,), s)

        def mult(q, u):
            c, g = q // 2, q % 2
            j, cc, b = c // 2, c % 2, 4 * g + u
            o = DBX(u).rearrange("p (a n t) -> p a n t", a=4, n=16)[:, :, :, 1:11]
            i0 = U(c)[:, :, b, :].unsqueeze(2).to_broadcast([128, 4, 16, 10])
            i1 = BB[:, q % 3, :, u, :].unsqueeze(1).to_broadcast([128, 4, 16, 10])
            k["m1", q] = k["m1", q, u] = put(DV, lambda: V.tensor_tensor(o, i0, i1, ALU.mult), (k["bb", q], k["u", c], k.get(("dbx", u % 2))), sem("m1"))

        def carry(q, u):
            o = PM[:, 640:640 + 2 * CH].rearrange("p (u a t) -> p u a t", u=2, t=11)[:, :, :, 0]
            w = [k.get(("dbx", 0)), k.get(("dbx", 1))]
            if q < 2:
                t = put(DV, lambda: V.memset(o, 0.0), w, sem("ca"))
            else:
                i = H[:, (q - 2) % 3, u:u + 2].rearrange("p u (a t) -> p u a t", t=11)[:, :, :, 10]
                f = FC[:, q % 2, u:u + 2].unsqueeze(2).to_broadcast([128, 2, 64])
                t = put(DV, lambda: V.tensor_tensor(o, i, f, ALU.mult), w + [k["fac", q]], sem("ca"))
            k["ca", q] = k["ca", q, u] = k["ca", q, u + 1] = t

        def scan(q, u):
            c, g = q // 2, q % 2
            a0 = DA[:, c % 4, 4 * g + u].rearrange("p a n t -> p (a n t)")
            k["scan", q] = put(DV, lambda: V.tensor_tensor_scan(
                H[:, q % 3, u], a0, DBX(u), 0.0, ALU.mult, ALU.add),
                (k["m1", q, u], k["ca", q, u], k["da", q], k.get(("ys", q - 3)), ze if q < 3 else None), sem("scan"))
            k["scan", q, u] = k["dbx", u % 2] = k["scan", q]

        def squared(q, u):
            g = q % 2
            h = H[:, q % 3, u].rearrange("p (a t) -> p a t", t=11)[:, :, 10]
            k["sqs", q] = put(DV, lambda: V.tensor_tensor_reduce(
                out=JK[:, u % 2], in0=h, in1=h, scale=1.0, scalar=0.0, op0=ALU.mult, op1=ALU.add,
                accum_out=SS[:, g, u:u + 1]), (k["scan", q, u], k.get(("nrm", q - 2)), k.get(("jk", u % 2))), sem("sqs"))
            k["jk", u % 2] = k["sqs", q]

        def hc(q, u):
            h = H[:, q % 3, u].rearrange("p (a n t) -> p a n t", a=4, n=16)[:, :, :, 0:10]
            i1 = CB[:, q % 3, :, u, :].unsqueeze(1).to_broadcast([128, 4, 16, 10])
            k["hc", q] = put(PO, lambda: G.tensor_tensor(h, h, i1, ALU.mult),
                             (k["scan", q, u], k["cb", q]), sem("hc"))

        def norm_sum(q):
            k["nrm", q] = mms([(NP(q % 2), ONE[:], SS[:, q % 2], True, True)],
                              (k["sqs", q], k.get(("nread", q - 2)), k.get(("z", q - 2))), sem("nrm"))

        def y_sum(q, n0, n1):
            if not 0 <= q < 2 * NC:
                return
            hv = H[:, q % 3].rearrange("p u (a n t) -> p u a n t", a=4, n=16)
            k["ys", q] = mms([(YP(q).rearrange("p (u a t) -> p u a t", u=4, a=4), ID[:], hv[:, :, :, n, 0:10],
                               n == 0, n == 15) for n in range(n0, n1)],
                             (k["hc", q], k.get(("z", q - 2)), k.get(("nread", q))), sem("ys"))

        def z_out(q):
            if not 0 <= q < 2 * NC:
                return
            c, g = q // 2, q % 2
            j, cc = c // 2, c % 2

            def vw(t):
                return t.rearrange("p a b t -> p b a t")
            o = vw(Z[:, :, 4 * g:4 * g + 4, 10 * cc:10 * cc + 10])
            yv = YP(q).rearrange("p (u a t) -> p u a t", u=4, a=4)
            t = put(DV, lambda: V.tensor_tensor(
                o, yv, vw(SG[:, j % 2, :, 4 * g:4 * g + 4, 10 * cc:10 * cc + 10]), ALU.mult),
                (k["ys", q], k.get(("op", j - 1)), k["sg", j], k.get(("sgh", j))), sem("zm"))
            k["z", q] = put(DV, lambda: V.tensor_tensor(
                o, o, vw(DX[:, j % 2, :, 4 * g:4 * g + 4, 10 * cc:10 * cc + 10]), ALU.add),
                (t, k["dx", j]), sem("z"))

        def load_res(i):
            if ok(i):
                for g in range(2):
                    for b in range(4):
                        k["xr", i] = put(SP, lambda g=g, b=b: Y.dma_start(
                            XR[20 * b:20 * b + 20, g, :], d["xp"][4 * g + b, T * i:T * i + T, :]),
                            (k.get(("v", i - 1)),), sem("xr"), dma=True)

        def out_proj(i):
            if ok(i):
                n, p, waits = bank()
                zf = Z[:].rearrange("p a b t -> p a (b t)")
                k["op", i] = mms([(p[0:80, 256 * g:256 * g + 256], zf[:, a, 80 * g:80 * g + 80], WO[:, a, :],
                                   a == 0, a == 3) for g in range(2) for a in range(4)],
                                 [k["z", 4 * i + 3], pre] + waits, sem("op"))
                k["opb", i] = (n, p)

        def residual(i):
            if ok(i):
                n, p = k["opb", i]
                k["v", i] = put(DV, lambda: V.scalar_tensor_tensor(
                    VV[:].rearrange("p a b -> p (a b)"), XR[:].rearrange("p a b -> p (a b)"), 2.0, p[0:80, :],
                    ALU.mult, ALU.add), (k["op", i], k["xr", i], k.get(("x2d", i - 1)), k.get(("tr", i - 1))),
                    sem("v"))
                bank_free[n].append(k["v", i])
                for g in range(2):
                    t = put(DV, lambda g=g: V.bn_stats(BN[:, g], VV[:, g]), (k["v", i],), sem("bn"))
                for g in range(2):
                    k["mv", i] = put(DV, lambda g=g: V.bn_aggr(MVR[:, g], BN[:, g]), (t,), sem("mv"))

        def ln_root(i):
            if ok(i):
                k["sd", i] = put(AC, lambda: S.activation(SD[:], MVR[:, :, 1], ACT.Ln, bias=CST[0:80, 1:2]),
                                 (k["mv", i], k.get(("x2", i - 1))), sem("sd"))

        def ln_inv(i):
            if ok(i):
                k["isd", i] = put(AC, lambda: S.activation(SD[:], SD[:], ACT.Exp, scale=-0.5), (k["sd", i],), sem("isd"))

        def ln_out(i):
            if ok(i):
                for g in range(2):
                    k["x2", i] = put(DV, lambda g=g: V.tensor_scalar(
                        VV[:, g], VV[:, g], MVR[:, g, 0:1], SD[:, g:g + 1], ALU.subtract, ALU.mult),
                        (k["isd", i],), sem("x2"))
                for g in range(2):
                    for b in range(4):
                        k["x2d", i] = put(SP, lambda g=g, b=b: Y.dma_start(
                            X2d[4 * g + b, T * i:T * i + T, :], VV[20 * b:20 * b + 20, g, :]),
                            (k["x2", i],), sem("x2d"), dma=True)

        def transposed(i):
            if ok(i):
                n, p, waits = bank()
                tok = None
                for g in range(2):
                    for a in range(2):
                        o = p[:, 80 * (2 * g + a):80 * (2 * g + a) + 80]
                        tok = put(PE, lambda o=o, g=g, a=a: M.transpose(
                            o, VV[:, g, 128 * a:128 * a + 128], ID[0:80, 0:80]),
                            [k["x2", i]] + waits if (g, a) == (0, 0) else (), sem("tr"))
                k["tr", i] = tok
                k["x2t", i] = put(AC, lambda: S.activation(X2T[:].rearrange("p a b -> p (a b)"), p[:, 0:320],
                                                           ACT.Copy), (tok, k.get(("lg", i - 1))), sem("x2t"))
                bank_free[n].append(k["x2t", i])

        def logits(i):
            if ok(i):
                n, p, waits = bank()
                k["lg", i] = mms([(p[0:80, 8 * g:8 * g + 8], X2T[:, 2 * g + a, :], WR[:, a, :], a == 0, a == 1)
                                  for g in range(2) for a in range(2)], [k["x2t", i]] + waits, sem("lg"))
                k["lgb", i] = (n, p)

        def logits_out(i):
            if ok(i):
                n, p = k["lgb", i]
                t = put(DV, lambda: V.tensor_copy(LGS[:].rearrange("p a b -> p (a b)"), p[0:80, 0:16]),
                        (k["lg", i], k.get(("lgd", i - 1))), sem("lgs"))
                bank_free[n].append(t)
                for g in range(2):
                    for b in range(4):
                        k["lgd", i] = put(SP, lambda g=g, b=b: Y.dma_start(
                            LGd[4 * g + b, T * i:T * i + T, :], LGS[20 * b:20 * b + 20, g, :]),
                            (t,), sem("lgd"), dma=True)

        def window(i):
            live = ok(i)
            if i == NB + 1:
                transposed(i - 2)
                logits(i - 2)
                logits_out(i - 2)
                return
            for s in range(16):
                r, u = s // 4, s % 4
                q = 4 * i + r
                if s == 0:
                    load_x(i + 4)
                    project(i + 2, 0, "br")
                    halo(i + 2)
                if s == 1:
                    dt_out(i + 1)
                if s == 2:
                    transposed(i - 2)
                if 2 <= s < 6:
                    conv(i + 2, s - 2)
                if s == 3:
                    project(i + 1, 512, "gate")
                if s == 4:
                    gate_tanh(i + 1)
                if s == 7:
                    gate(i + 1)
                    out_proj(i - 1)
                    logits(i - 2)
                    if live:
                        dt_x(2 * i + 1)
                if s == 8:
                    gate_d(i + 1)
                if s == 9:
                    silu(i + 2)
                    logits_out(i - 2)
                    residual(i - 1)
                    load_res(i)
                    dt_proj(i + 2)
                    squares(i + 3)
                if s == 12:
                    softplus_log(i + 2)
                    roots(i + 3)
                    ln_root(i - 1)
                    bc_out(i + 2)
                    inv_roots(i + 3)
                    ln_inv(i - 1)
                if s == 14:
                    softplus(i + 2)
                    dt_tanh(i + 2)
                if s == 15:
                    normed(i + 3)
                    ln_out(i - 1)
                if 1 <= s < 12:
                    decay_tanh(i + 1, 6 * s - 6, 6 * s)
                elif s > 11:
                    decay_exp(i + 1, s - 12)
                if s == 1:
                    branch_out(i + 2)
                if s == 8:
                    silu_tanh(i + 2)
                if s == 11:
                    dt_bias(i + 2)
                    bc_proj(i + 2)
                    sum_squares(i + 3)
                if u == 0:
                    if live:
                        if r == 0:
                            dt_x(q // 2)
                if u == 0:
                    y_sum(q - 2, 11, 16)
                if u == 3:
                    y_sum(q - 1, 6, 11)
                if live:
                    if u % 2 == 0:
                        mult(q, u)
                        if u == 0:
                            rest(DV)
                        carry(q, u)
                        mult(q, u + 1)
                    scan(q, u)
                    hc(q, u)
                if u == 2:
                    z_out(q - 2)
                    if 0 <= q - 1 < 2 * NC - 2:
                        assert ("nread", q - 1) in k
                    y_sum(q - 1, 0, 6)
                if live:
                    if u > 0:
                        squared(q, u - 1)
                    if u == 1 and 1 <= q < 2 * NC - 1:
                        side = factor(q + 1)
                        next(side)
                        DV.side = side
                    if u == 3:
                        squared(q, 3)
                        norm_sum(q)
                if u == 3 and q + 2 >= 0:
                    bring(q + 2)

        for i in range(-4, NB + 2):
            window(i)
        for name in ("x2d", "lgd", "xe0", "bd0", "cd0", "bd1", "cd1"):
            if name in sems:
                put(SP, None, ((sems[name], sems[name].n),))
        run_block(nc, qs)


def moe_phase(nc, d, XE, X2d, LGd, YO, out):
    ctx = ExitStack()
    with ctx:
        def sb(name, shape, dt=F32):
            return ctx.enter_context(nc.sbuf_tensor(name, shape, dt))

        sems = {}

        def sem(name):
            if name not in sems:
                sems[name] = Sem(ctx.enter_context(nc.semaphore("m_" + name)))
            return sems[name]

        qs = {k: Queue() for k in ("sp", "act", "dve", "pool", "pe")}
        SP, AC, DV, PO, PE = qs["sp"], qs["act"], qs["dve"], qs["pool"], qs["pe"]
        V, S, G, M, Y = nc.vector, nc.scalar, nc.gpsimd, nc.tensor, nc.sync

        X2 = sb("X2", [128, 64, 256])
        W1 = sb("W1", [128, 2, 2, 1024])
        W2 = sb("W2", [128, 2, 8, 256])
        B1 = sb("B1", [128, 8, 8])
        B2 = sb("B2", [128, 8, 256])
        XR = sb("XRE", [128, 2, 6, 256])
        XT = sb("XTE", [128, 2, 768])
        HT = sb("HT", [128, 8, 768])
        YS = sb("YS", [128, 2, 2, 256])
        GA = sb("GA", [128, 4, 2, 256])
        ID = sb("ID2", [128, 128])
        ONE = sb("ONE2", [128, 128])
        TRI = sb("TRI", [128, 128])
        IO = sb("IO", [128, 8])
        LG = sb("LG", [128, 64, 8])
        P = sb("P", [128, 64, 8])
        VL = sb("VL", [128, 64, 8])
        OH = sb("OH", [128, 2, 64, 8])
        MM = sb("MM", [128, 64, 8])
        CN = sb("CN", [128, 8, 64])
        MK = sb("MK", [128, 8, 64])
        CI = sb("CI", [128, 8, 64])
        PO_ = sb("POS", [128, 64, 8])
        R = sb("R", [128, 16, 64])
        IX = sb("IX", [128, 4, 64], I32)
        BN = sb("BN2", [128, 4, 6])
        MV = sb("MV2", [128, 4, 2])
        SD = sb("SD2", [128, 4])
        EP = sb("EP", [128, 1])
        PB = [ctx.enter_context(nc.psum_tensor(f"PE{i}", [128, 512], F32)) for i in range(8)]

        k = {}
        lg = put(SP, lambda: Y.dma_start(ID[:], d["ident"]), (), sem("ld"), dma=True)
        lg = put(SP, lambda: Y.dma_start(TRI[:], d["tri"]), (), sem("ld"), dma=True)
        lg = put(SP, lambda: Y.dma_start(IO[:], d["iota"].to_broadcast([128, 8])), (), sem("ld"), dma=True)
        for b in range(8):
            lg = put(SP, lambda b=b: Y.dma_start(
                LG[:, 8 * b:8 * b + 8, :], LGd[b, 10:10 + L, :].rearrange("(j p) e -> p j e", p=128)),
                (), sem("ld"), dma=True)
        for b in range(8):
            k["x2", b] = put(SP, lambda b=b: Y.dma_start(
                X2[:, 8 * b:8 * b + 8, :], X2d[b, 10:10 + L, :].rearrange("(j p) n -> p j n", p=128)),
                (), sem(f"x2l{b}"), dma=True)
        put(AC, lambda: S.dma_start(B1[:], d["b1"]), (), sem("bl"), dma=True)
        bl = put(AC, lambda: S.dma_start(B2[:].rearrange("p e n -> p (e n)"),
                                         d["b2"].rearrange("e n -> (e n)").partition_broadcast(128)),
                 (), sem("bl"), dma=True)

        s = sem("rt")

        def dv(fn, *waits):
            k["c"] = put(DV, fn, (k.get("c"),) + waits, s)
            return k["c"]

        def bc(t):
            return t.unsqueeze(2).to_broadcast([128, 64, 8])

        dv(lambda: V.memset(ONE[:], 1.0))
        dv(lambda: V.memset(EP[:], 1e-5))
        dv(lambda: V.memset(MK[:], 1.0))
        dv(lambda: V.memset(MK[:, :, 0:1], 0.0))
        dv(lambda: V.tensor_reduce(R[:, 0], LG[:], AX.X, ALU.max), lg)
        t = dv(lambda: V.tensor_tensor(P[:], LG[:], bc(R[:, 0]), ALU.subtract))
        a = put(AC, lambda: S.activation(P[:], P[:], ACT.Exp), (t,), sem("ra"))
        dv(lambda: V.tensor_reduce(R[:, 1], P[:], AX.X, ALU.add), a)
        dv(lambda: V.reciprocal(R[:, 1], R[:, 1]))
        dv(lambda: V.tensor_tensor(P[:], P[:], bc(R[:, 1]), ALU.mult))
        for n in range(2):
            pk, ek = R[:, 2 + n], R[:, 4 + n]
            iob = IO[:].unsqueeze(1).to_broadcast([128, 64, 8])
            dv(lambda pk=pk: V.tensor_reduce(pk, P[:], AX.X, ALU.max))
            dv(lambda pk=pk: V.tensor_tensor(VL[:], P[:], bc(pk), ALU.is_ge))
            dv(lambda: V.scalar_tensor_tensor(VL[:], VL[:], -100.0, iob, ALU.mult, ALU.add))
            dv(lambda ek=ek: V.tensor_reduce(ek, VL[:], AX.X, ALU.min))
            dv(lambda ek=ek, n=n: V.tensor_tensor(OH[:, n], VL[:], bc(ek), ALU.is_equal))
            if n == 0:
                dv(lambda: V.scalar_tensor_tensor(P[:], OH[:, 0], -4.0, P[:], ALU.mult, ALU.add))
        t = dv(lambda: V.tensor_tensor(MM[:], OH[:, 0], OH[:, 1], ALU.add))
        put(PE, lambda: M.matmul(PB[0][:], TRI[:], MM[:].rearrange("p j e -> p (j e)"), start=True, stop=True),
            (t, lg), sem("rp"))
        t = put(PE, lambda: M.matmul(PB[1][:], ONE[:], MM[:].rearrange("p j e -> p (j e)"), start=True, stop=True),
                (), sem("rp"))
        dv(lambda: V.tensor_copy(CN[:], PB[1][:].rearrange("p (j e) -> p e j", e=8)), t)
        dv(lambda: V.tensor_tensor_scan(CI[:].rearrange("p e j -> p (e j)"), MK[:].rearrange("p e j -> p (e j)"),
                                        CN[:].rearrange("p e j -> p (e j)"), 0.0, ALU.mult, ALU.add))
        dv(lambda: V.tensor_tensor(CI[:], CI[:], CN[:], ALU.subtract))
        dv(lambda: V.tensor_tensor(PO_[:], PB[0][:].rearrange("p (j e) -> p j e", e=8),
                                   CI[:].rearrange("p e j -> p j e"), ALU.add))
        dv(lambda: V.tensor_tensor(R[:, 6], R[:, 2], R[:, 3], ALU.add))
        dv(lambda: V.reciprocal(R[:, 6], R[:, 6]))
        for n in range(2):

            dv(lambda n=n: V.tensor_tensor(VL[:], PO_[:], OH[:, n], ALU.mult))
            dv(lambda: V.tensor_reduce(R[:, 7], VL[:], AX.X, ALU.add))
            dv(lambda n=n: V.tensor_scalar(R[:, 8 + n], R[:, 7], float(CAP), None, ALU.is_lt))
            dv(lambda n=n: V.tensor_scalar(R[:, 10], R[:, 4 + n], 100.0, float(CAP), ALU.add, ALU.mult))
            dv(lambda n=n: V.tensor_scalar(R[:, 11], R[:, 8 + n], -100000.0, 100000.0, ALU.mult, ALU.add))
            dv(lambda: V.tensor_tensor(R[:, 11], R[:, 11], R[:, 7], ALU.add))
            dv(lambda: V.tensor_tensor(R[:, 11], R[:, 11], R[:, 10], ALU.add))
            k["sc"] = dv(lambda n=n: V.tensor_copy(IX[:, n], R[:, 11]))
            dv(lambda n=n: V.tensor_tensor(R[:, 7], R[:, 7], R[:, 8 + n], ALU.mult))
            dv(lambda: V.tensor_tensor(R[:, 7], R[:, 7], R[:, 10], ALU.add))
            dv(lambda n=n: V.tensor_copy(IX[:, 2 + n], R[:, 7]))
            dv(lambda n=n: V.tensor_tensor(R[:, 12 + n], R[:, 2 + n], R[:, 6], ALU.mult))
            k["g"] = dv(lambda n=n: V.tensor_tensor(R[:, 12 + n], R[:, 12 + n], R[:, 8 + n], ALU.mult))

        for j in range(64):
            for n in range(2):
                k["disp"] = put(PO, lambda j=j, n=n: G.indirect_dma_start(
                    out=XE, out_offset=bass.IndirectOffsetOnAxis(ap=IX[:, n, j:j + 1].bitcast(U32), axis=0),
                    in_=X2[:, j, :], in_offset=None, bounds_check=E * CAP - 1, oob_is_err=False),
                    (k["g"], k["x2", j // 8]), sem("disp"), dma=True)

        def load_w(e):
            if e < E:
                put(AC, lambda: S.dma_start(W1[:, e % 2], d["w1"][e].rearrange("(a p) n -> p a n", p=128)),
                    (k.get(("h", e - 2)),), sem(f"wl{e % 2}"), dma=True)
                k["w", e] = put(AC, lambda: S.dma_start(W2[:, e % 2], d["w2"][e].rearrange("(a p) n -> p a n", p=128)),
                                (k.get(("y", e - 2)),), sem(f"wl{e % 2}"), dma=True)

        def load_e(e):
            if e < E:
                k["xe", e] = put(SP, lambda: Y.dma_start(
                    XR[:, e % 2], XE[e * CAP:(e + 1) * CAP, :].rearrange("(s p) n -> p s n", p=128)),
                    (k["disp"], k.get(("xt", e - 2))), sem(f"xe{e % 2}"), dma=True)

        free = {}
        nb = [2]

        def bank():
            n = nb[0] % 8
            nb[0] += 1
            return n, PB[n], [free.get(n)]

        load_w(0)
        load_w(1)
        load_e(0)
        load_e(1)
        for e in range(E):
            for c in range(3):
                n, p, waits = bank()
                for a in range(2):
                    for h in range(2):
                        o = p[:, 256 * a + 128 * h:256 * a + 128 * h + 128]
                        t = put(PE, lambda o=o, a=a, h=h, c=c, e=e: M.transpose(
                            o, XR[:, e % 2, 2 * c + h, 128 * a:128 * a + 128], ID[:]),
                            waits + [k["xe", e], lg, k["g"]], sem("xt"))
                free[n] = put(DV, lambda p=p, c=c: V.tensor_copy(
                    XT[:, :, 256 * c:256 * c + 256], p[:].rearrange("p (a n) -> p a n", a=2)),
                    (t, k.get(("h", e - 1))), sem("xtc"))
            k["xt", e] = t
            xc = free[n]
            load_e(e + 2)
            for m in range(8):
                for h in range(2):
                    n, p, waits = bank()
                    for a in range(2):
                        t = put(PE, lambda p=p, a=a, m=m, h=h, e=e: M.matmul(
                            p[:, 0:384], W1[:, e % 2, a, 128 * m:128 * m + 128], XT[:, a, 384 * h:384 * h + 384],
                            start=a == 0, stop=a == 1), waits + [xc, k["w", e]], sem("h"))
                    if h == 0:
                        free[n] = r0 = put(AC, lambda p=p, m=m, h=h, e=e: S.activation(
                            HT[:, m, 384 * h:384 * h + 384], p[:, 0:384], ACT.Relu, bias=B1[:, e, m:m + 1]),
                            (t, bl, k.get(("y", e - 1))), sem("ra"))
                    else:
                        free[n] = r1 = put(DV, lambda p=p, m=m, h=h, e=e: V.tensor_scalar(
                            HT[:, m, 384 * h:384 * h + 384], p[:, 0:384], B1[:, e, m:m + 1], 0.0,
                            ALU.add, ALU.max), (t, bl, k.get(("y", e - 1))), sem("rv"))
            k["h", e] = t
            for c in range(3):
                n, p, waits = bank()
                for h in range(2):
                    for m in range(8):
                        t = put(PE, lambda p=p, m=m, h=h, c=c, e=e: M.matmul(
                            p[:, 256 * h:256 * h + 256], HT[:, m, 128 * (2 * c + h):128 * (2 * c + h) + 128],
                            W2[:, e % 2, m, :], start=m == 0, stop=m == 7), waits + [r0, r1], sem("y"))
                i = 3 * e + c
                free[n] = t2 = put(DV, lambda p=p, i=i, e=e: V.tensor_tensor(
                    YS[:, i % 2], p[:].rearrange("p (h n) -> p h n", h=2),
                    B2[:, e].unsqueeze(1).to_broadcast([128, 2, 256]), ALU.add),
                    (t, k.get(("yo", i - 2))), sem("ys"))
                k["yo", i] = put(SP, lambda i=i: Y.dma_start(
                    YO[256 * i:256 * i + 256, :].rearrange("(h p) n -> p h n", p=128), YS[:, i % 2]),
                    (t2,), sem(f"yo{i % 2}"), dma=True)
            k["y", e] = t
            load_w(e + 2)

        yo = (k["yo", 22], k["yo", 23])

        def gather(j):
            for n in range(2):
                k["ga", j] = put(PO, lambda n=n: G.indirect_dma_start(
                    out=GA[:, j % 4, n], out_offset=None, in_=YO,
                    in_offset=bass.IndirectOffsetOnAxis(ap=IX[:, 2 + n, j:j + 1].bitcast(U32), axis=0),
                    bounds_check=E * CAP - 1, oob_is_err=False), yo + (k.get(("a", j - 4)),),
                    sem(f"ga{j % 4}"), dma=True)

        def combine(j):
            t = put(DV, lambda: V.scalar_tensor_tensor(
                X2[:, j], GA[:, j % 4, 0], R[:, 12, j:j + 1], X2[:, j], ALU.mult, ALU.add),
                (k["ga", j], k["disp"]), sem("ca"))
            k["a", j] = t = put(DV, lambda: V.scalar_tensor_tensor(
                X2[:, j], GA[:, j % 4, 1], R[:, 13, j:j + 1], X2[:, j], ALU.mult, ALU.add), (t,), sem("ca"))
            t = put(DV, lambda: V.bn_stats(BN[:, j % 4], X2[:, j]), (t, k.get(("mv", j - 4))), sem("ca"))
            k["mv", j] = put(DV, lambda: V.bn_aggr(MV[:, j % 4], BN[:, j % 4]), (t, k.get(("x3", j - 4))), sem("ca"))
            k["sd", j] = put(AC, lambda: S.activation(SD[:, j % 4:j % 4 + 1], MV[:, j % 4, 1:2], ACT.Sqrt,
                                                      bias=EP[:]), (k["mv", j],), sem("sd"))

        def finish(j):
            t = put(DV, lambda: V.reciprocal(SD[:, j % 4:j % 4 + 1], SD[:, j % 4:j % 4 + 1]), (k["sd", j],), sem("ca"))
            k["x3", j] = put(DV, lambda: V.tensor_scalar(X2[:, j], X2[:, j], MV[:, j % 4, 0:1],
                                                         SD[:, j % 4:j % 4 + 1], ALU.subtract, ALU.mult),
                             (t,), sem("ca"))
            k["out"] = put(SP, lambda: Y.dma_start(out[128 * j:128 * j + 128, :], X2[:, j]), (k["x3", j],),
                           sem("out"), dma=True)

        for j in range(64 + 1):
            if j < 64:
                gather(j)
                combine(j)
            if j >= 1:
                finish(j - 1)
        put(SP, None, (k["out"],))
        run_block(nc, qs)


def build(nc, d, out):
    XE = nc.dram_tensor("XE", [E * CAP, DM], F32, kind="Internal").ap()
    YO = nc.dram_tensor("YO", [E * CAP, DM], F32, kind="Internal").ap()
    X2d = nc.dram_tensor("X2d", [B, LP, DM], F32, kind="Internal").ap()
    LGd = nc.dram_tensor("LGd", [B, LP, E], F32, kind="Internal").ap()
    Bd = nc.dram_tensor("Bd", [NC, 2, NS, 40], F32, kind="Internal").ap()
    Cd = nc.dram_tensor("Cd", [NC, 2, NS, 40], F32, kind="Internal").ap()
    ssm_phase(nc, d, XE, X2d, LGd, Bd, Cd)
    moe_phase(nc, d, XE, X2d, LGd, YO, out)


def kernel(**inputs):
    import concourse.bacc as bacc
    from concourse.bass_utils import run_bass_kernel_spmd

    a = {n: np.asarray(v) for n, v in inputs.items()}
    x = a["L0_attn_x"]
    xp = np.zeros((B, LP + 1, DM), np.float32)
    xp[:, 10:10 + L] = x
    xT = xp[:, 1:].reshape(B, NB, T, 2, 128).transpose(1, 4, 3, 0, 2).reshape(NB, 128, 2, B * T)
    wbc = np.zeros((DI, 64), np.float32)
    wbc[:, 0:16] = a["L0_attn_W_B"].T
    wbc[:, 32:48] = a["L0_attn_W_C"].T
    arrays = {
        "xT": xT, "xp": xp[:, :LP],
        "w_in": a["L0_attn_W_in"].T, "w_dt": a["L0_attn_W_dt"].T, "w_bc": wbc, "w_out": a["L0_attn_W_out"].T,
        "a_log": a["L0_attn_A_log"], "conv_w": a["L0_attn_conv_w"].reshape(DI, 4), 
        "vecs": np.stack([a[n].reshape(4, 128).T for n in ("L0_attn_conv_b", "L0_attn_b_dt", "L0_attn_D_param")], 1),
        "norm_w": a["L0_attn_norm_w"].reshape(2, 128).T,
        "res": a["L0_attn_residual_scale"].reshape(1, 1), "w_router": a["L0_ffn_w_router"],
        "w1": a["L0_ffn_w1"], "b1": a["L0_ffn_b1"].reshape(E, 8, 128).transpose(2, 0, 1), "w2": a["L0_ffn_w2"], "b2": a["L0_ffn_b2"],
        "ident": np.eye(128, dtype=np.float32), "tri": np.triu(np.ones((128, 128), np.float32), 1),
        "iota": np.arange(8, dtype=np.float32).reshape(1, 8),
    }
    nc = bacc.Bacc("TRN2", target_bir_lowering=False, num_devices=1)
    feed, d = {}, {}
    for n, v in arrays.items():
        v = np.ascontiguousarray(v)
        feed[f"in_{n}"] = v
        d[n] = nc.dram_tensor(f"in_{n}", v.shape, mybir.dt.from_np(v.dtype), kind="ExternalInput").ap()
    out = nc.dram_tensor("out_y", [B * L, DM], F32, kind="ExternalOutput").ap()
    build(nc, d, out)
    r = run_bass_kernel_spmd(nc, [feed], core_ids=[0])
    return r.results[0]["out_y"].reshape(B, L, DM)
```

```python
import numpy as np
import concourse.bass as bass
from concourse import mybir
from contextlib import ExitStack

F32 = mybir.dt.float32
I32 = mybir.dt.int32
U32 = mybir.dt.uint32
ALU = mybir.AluOpType
ACT = mybir.ActivationFunctionType
AX = mybir.AxisListType

B, L, DM, DI, NS = 8, 1024, 256, 512, 16
E, HF, CAP = 8, 1024, 768
T = 20
NB = 52
LP = NB * T
NC = 2 * NB
CH = 704


class Queue:

    def __init__(self):
        self.items = []
        self.side = None

    def play(self, eng):
        seen = {}
        for waits, fn, sem, inc in self.items:
            for s, v in waits:
                if seen.get(s, 0) < v:
                    eng.wait_ge(s.h, v)
                    seen[s] = v
            if fn is None:
                continue
            ins = fn()
            if sem is not None:
                ins.then_inc(sem.h, inc)


class Sem:

    def __init__(self, h):
        self.h, self.n = h, 0


def put(q, fn, waits=(), sem=None, dma=False):
    inc = 16 if dma else 1
    tok = None
    if sem is not None:
        sem.n += inc
        tok = (sem, sem.n)
    q.items.append(([w for w in waits if w is not None], fn, sem, inc))
    if q.side is not None:
        side, q.side = q.side, None
        if next(side, True) is None:
            q.side = side
    return tok


def rest(q):
    side, q.side = q.side, None
    for _ in side or ():
        pass


def run_block(nc, qs):
    with nc.Block() as block:
        @block.sync
        def _(eng):
            qs["sp"].play(eng)

        @block.scalar
        def _(eng):
            qs["act"].play(eng)

        @block.vector
        def _(eng):
            qs["dve"].play(eng)

        @block.gpsimd
        def _(eng):
            qs["pool"].play(eng)

        @block.tensor
        def _(eng):
            qs["pe"].play(eng)


def ssm_phase(nc, d, YA, X2d, LGd, Bd, Cd):
    ctx = ExitStack()
    with ctx:
        def sb(name, shape, dt=F32):
            return ctx.enter_context(nc.sbuf_tensor(name, shape, dt))

        sems = {}

        def sem(name):
            if name not in sems:
                sems[name] = Sem(ctx.enter_context(nc.semaphore(name)))
            return sems[name]

        qs = {k: Queue() for k in ("sp", "act", "dve", "pool", "pe")}
        SP, AC, DV, PO, PE = qs["sp"], qs["act"], qs["dve"], qs["pool"], qs["pe"]
        V, S, G, M, Y = nc.vector, nc.scalar, nc.gpsimd, nc.tensor, nc.sync

        DA = sb("DA", [128, 4, 8, 4, 16, 11])
        H = sb("H", [128, 3, 4, CH])
        BB = sb("BB", [128, 3, 16, 4, 10])
        CB = sb("CB", [128, 3, 16, 4, 10])
        WIN = sb("WIN", [128, 2, 1024])
        WDT = sb("WDT", [128, 4, 512])
        WBC = sb("WBC", [128, 4, 64])
        WO = sb("WO", [128, 4, 256])
        WR = sb("WR", [128, 2, 8])
        ID = sb("ID", [128, 128])
        ONE = sb("ONE", [128, 128])
        MEAN = sb("MEAN", [128, 128])
        AS = sb("AS", [128, 4, 16])
        CW = sb("CW", [128, 4, 4])
        PV = sb("PV", [128, 3, 4])
        NW = sb("NW", [128, 2])
        SC = sb("SC", [128, 2])
        CST = sb("CST", [128, 4])
        XT = sb("XT", [128, 2, 2, 160])
        XN = sb("XN", [128, 2, 2, 160])
        RST = sb("RST", [128, 160])
        XB = sb("XB", [128, 4, 8, 23])
        TA = sb("TA", [128, 4, 8, 20])
        TB = sb("TB", [128, 4, 8, 20])
        TC = sb("TC", [128, 4, 8, 20])
        XC = sb("XC", [128, 2, 4, 8, 20])
        DT = sb("DT", [128, 2, 4, 8, 20])
        SG = sb("SG", [128, 2, 4, 8, 21])
        DX = sb("DX", [128, 2, 4, 8, 21])
        Z = sb("Z", [128, 4, 8, 20])
        BS = sb("BS", [16, 2, 8, 10])
        CS = sb("CS", [64, 4, 8, 10])
        XR = sb("XR", [80, 2, 256])
        VV = sb("VV", [80, 2, 256])
        BN = sb("BN", [80, 2, 6])
        MVR = sb("MVR", [80, 2, 2])
        SD = sb("SD", [80, 2])
        X2T = sb("X2T", [128, 4, 80])
        LGS = sb("LGS", [80, 2, 8])
        SS = sb("SS", [128, 2, 4])
        JK = sb("JK", [128, 2, 64])
        FW = sb("FW", [128, 2, 4, 4])
        FI = sb("FI", [128, 2, 4], I32)
        FC = sb("FC", [128, 2, 4])
        PM = ctx.enter_context(nc.psum_tensor("PM", [128, 2048], F32))
        PB = [ctx.enter_context(nc.psum_tensor(f"PB{i}", [128, 512], F32)) for i in range(2)]

        YB = [ctx.enter_context(nc.psum_tensor(f"YB{i}", [128, 512], F32)) for i in range(2)]

        def U(c):
            return PM[:, 320 * (c % 2):320 * (c % 2) + 320].rearrange("p (a b t) -> p a b t", a=4, b=8)

        def DBX(u):
            return PM[:, 640 + CH * (u % 2):640 + CH * (u % 2) + CH]

        def YP(q):
            return YB[q % 2][:, 0:160]

        def NP(g):
            return YB[g][:, 256:260]

        w = []
        for k, (dst, src) in enumerate([
                (WIN[:], d["w_in"].rearrange("(a p) n -> p a n", p=128)),
                (WDT[:], d["w_dt"].rearrange("(a p) n -> p a n", p=128)),
                (WBC[:], d["w_bc"].rearrange("(a p) n -> p a n", p=128)),
                (WO[:], d["w_out"].rearrange("(a p) n -> p a n", p=128)),
                (WR[:], d["w_router"].rearrange("(a p) n -> p a n", p=128)),
                (ID[:], d["ident"]),
                (AS[:], d["a_log"].rearrange("(a p) n -> p a n", p=128)),
                (CW[:], d["conv_w"].rearrange("(a p) n -> p a n", p=128)),
                (PV[:], d["vecs"]),
                (NW[:], d["norm_w"]),
                (SC[:, 0:1], d["res"].to_broadcast([128, 1])),
        ]):
            w.append(put(AC, lambda dst=dst, src=src: S.dma_start(dst, src), (), sem("w_load"), dma=True))
        wall = w[-1]
        s_pre = sem("pre")
        c1 = put(DV, lambda: V.memset(ONE[:], 1.0), (), s_pre)
        c1 = put(DV, lambda: V.memset(MEAN[:], 1.0 / 256), (), s_pre)
        KD = 0.5 / (0.0495 + 1e-8)
        for col, val in enumerate((1e-6, 1e-5, -0.0505 * KD, 0.0)):
            c1 = put(DV, lambda col=col, val=val: V.memset(CST[:, col:col + 1], val), (), s_pre)
        c1 = put(DV, lambda: V.memset(XB[:], 0.0), (), s_pre)
        c1 = put(DV, lambda: V.memset(CS[:], 0.0), (), s_pre)
        c1 = put(DV, lambda: V.memset(SG[:], 0.0), (), s_pre)
        c1 = put(DV, lambda: V.memset(DX[:], 0.0), (), s_pre)
        c1 = put(DV, lambda: V.memset(DA[:, :, :, :, :, 0:1].rearrange("p c b a n t -> p (c b a n) t"), 0.0), (), s_pre)
        z0 = put(PO, lambda: G.memset(H[:], 0.0), (), sem("h0"))
        ROWS = H[:].rearrange("p a b c -> p (a b c)")
        YR = YA.rearrange("(p r) n -> p (r n)", p=128)
        for f, n in ((0, 33 * 256), (33 * 256, 32 * 256)):
            ze = put(SP, lambda f=f, n=n: Y.dma_start(YR[:, f:f + n], ROWS[:, 0:n]), (z0,), sem("ya0"), dma=True)
        c1 = put(DV, lambda: V.tensor_scalar(CW[:], CW[:], 0.5, None, ALU.mult), (wall,), s_pre)
        c1 = put(DV, lambda: V.tensor_scalar(PV[:, 0, :], PV[:, 0, :], 0.5, None, ALU.mult), (), s_pre)
        a1 = put(AC, lambda: S.activation(AS[:], AS[:], ACT.Tanh, scale=0.5 / (5.0 + 1e-8)), (wall,), sem("pre_a"))
        a1 = put(AC, lambda: S.activation(AS[:], AS[:], ACT.Exp, scale=10.0), (a1,), sem("pre_a"))
        c1 = put(DV, lambda: V.tensor_scalar(AS[:], AS[:], -0.5 / (8.0 + 1e-8), None, ALU.mult), (a1,), s_pre)
        a1 = put(AC, lambda: S.activation(SC[:, 1:2], SC[:, 0:1], ACT.Tanh, scale=0.5), (), sem("pre_a"))
        c1 = put(DV, lambda: V.tensor_scalar(SC[:, 0:1], SC[:, 1:2], 0.125, 0.125, ALU.mult, ALU.add), (a1,), s_pre)
        pre = put(DV, lambda: V.tensor_scalar(WO[:], WO[:], SC[:, 0:1], None, ALU.mult), (c1,), s_pre)

        k = {}
        bank_free = [[None], [None]]
        nbank = [0]

        def bank():
            n = nbank[0] % 2
            nbank[0] += 1
            assert bank_free[n]
            waits, bank_free[n] = bank_free[n], []
            return n, PB[n], waits

        def mms(specs, waits, s):
            tok = None
            for n, (o, l, r, st, sp) in enumerate(specs):
                tok = put(PE, lambda o=o, l=l, r=r, st=st, sp=sp: M.matmul(o, l, r, start=st, stop=sp),
                          waits if n == 0 else (), s if n == len(specs) - 1 else None)
            return tok

        def ok(j):
            return 0 <= j < NB

        def load_x(j):
            if ok(j):
                k["xt", j] = put(SP, lambda: Y.dma_start(XT[:, j % 2], d["xT"][j]),
                                 (k.get(("xn", j - 2)), k.get(("sq", j - 2))), sem(f"xt{j % 2}"), dma=True)

        def squares(j):
            if ok(j):
                k["sq", j] = put(AC, lambda: S.activation(XN[:, j % 2], XT[:, j % 2], ACT.Square),
                                 (k["xt", j], k.get(("gate", j - 2))), sem("sq"))

        def sum_squares(j):
            if ok(j):
                n, p, waits = bank()
                sq = XN[:, j % 2]
                k["ssum", j] = mms([(p[:, 0:160], MEAN[:], sq[:, 0], True, False),
                                    (p[:, 0:160], MEAN[:], sq[:, 1], False, True)],
                                   [k["sq", j], pre] + waits, sem("ssum"))
                k["rt", j] = (n, p)

        def roots(j):
            if ok(j):
                n, p = k["rt", j]
                k["root", j] = put(AC, lambda: S.activation(RST[:], p[:, 0:160], ACT.Ln, bias=CST[:, 0:1]),
                                   (k["ssum", j], k.get(("xn", j - 1)), pre), sem("root"))
                bank_free[n].append(k["root", j])

        def inv_roots(j):
            if ok(j):
                k["rs", j] = put(AC, lambda: S.activation(RST[:], RST[:], ACT.Exp, scale=-0.5),
                                 (k["root", j],), sem("rs"))

        def normed(j):
            if ok(j):
                for a in range(2):
                    k["xn", j] = put(DV, lambda a=a: V.scalar_tensor_tensor(
                        XN[:, j % 2, a], XT[:, j % 2, a], NW[:, a:a + 1], RST[:], ALU.mult, ALU.mult),
                        (k["rs", j],), sem("xn"))

        def halo(j):
            if ok(j) and j > 0:
                k["halo", j] = put(PO, lambda: G.tensor_copy(XB[:, :, :, 0:3], XB[:, :, :, 20:23]),
                                   (k["conv", j - 1],), sem("halo"))

        def project(j, first, name):
            if not ok(j):
                return
            out = []
            for m in range(2):
                n, p, waits = bank()
                sp = []
                for a in range(2):
                    c = first + 256 * m + 128 * a
                    for kk in range(2):
                        sp.append((p[:, 160 * a:160 * a + 160], WIN[:, kk, c:c + 128], XN[:, j % 2, kk],
                                   kk == 0, kk == 1))
                tok = mms(sp, [k["xn", j]] + waits, sem("proj"))
                out.append((n, p, tok))
            k[name, j] = tok
            k[name + "_b", j] = out

        def branch_out(j):
            if ok(j):
                for m, (n, p, tok) in enumerate(k["br_b", j]):
                    k["xb", j] = put(AC, lambda m=m, p=p: S.activation(
                        XB[:, 2 * m:2 * m + 2, :, 3:23], p[:, 0:320].rearrange("p (a b t) -> p a b t", a=2, b=8),
                        ACT.Copy), (tok, k.get(("halo", j)), k.get(("conv", j - 1)), pre), sem("xb"))
                    bank_free[n].append(k["xb", j])

        def conv(j, part):
            if not ok(j):
                return
            sc = sem("conv")
            if part == 0:
                for a in range(4):
                    k["cv", j] = put(PO, lambda a=a: G.tensor_scalar(
                        TA[:, a], XB[:, a, :, 0:20], CW[:, a, 0:1], PV[:, 0, a:a + 1], ALU.mult, ALU.add),
                        (k["xb", j], k.get(("halo", j)), k.get(("dt", j - 1)), pre), sc)
            if part > 0:
                k["conv", j] = k["cv", j] = put(PO, lambda: G.tensor_tensor(TA[:], TA[:], TC[:], ALU.add),
                                                (k["ct", j],), sc)
            if part < 3:
                tap = part + 1
                wv = CW[:, :, tap:tap + 1].unsqueeze(3).to_broadcast([128, 4, 8, 20])
                k["ct", j] = put(PO, lambda: G.tensor_tensor(TC[:], XB[:, :, :, tap:tap + 20], wv, ALU.mult),
                                 (k["cv", j], k.get(("dx", j - 2))), sc)

        def silu_tanh(j):
            if ok(j):
                k["th", j] = put(AC, lambda: S.activation(TB[:], TA[:], ACT.Tanh),
                                 (k["conv", j], k.get(("sg", j - 1))), sem("th"))

        def silu(j):
            if ok(j):
                k["xc", j] = put(DV, lambda: V.scalar_tensor_tensor(
                    XC[:, j % 2].rearrange("p a b t -> p (a b t)"), TB[:].rearrange("p a b t -> p (a b t)"), 1.0,
                    TA[:].rearrange("p a b t -> p (a b t)"), ALU.add, ALU.mult),
                    (k["th", j], k.get(("bc", j - 2)), k.get(("dx", j - 2)), k.get(("u", 2 * j - 3))), sem("xc"))

        def dt_proj(j):
            if not ok(j):
                return
            out = []
            for m in range(2):
                n, p, waits = bank()
                sp = []
                for a in range(2):
                    c = 256 * m + 128 * a
                    for kk in range(4):
                        sp.append((p[:, 160 * a:160 * a + 160], WDT[:, kk, c:c + 128],
                                   XC[:, j % 2, kk].rearrange("p b t -> p (b t)"), kk == 0, kk == 3))
                out.append((n, p, mms(sp, [k["xc", j]] + waits, sem("dtp"))))
            k["dtp", j] = out

        def bc_proj(j):
            if not ok(j):
                return
            n, p, waits = bank()
            k["bc", j] = mms([(p[0:64, 0:160], WBC[:, kk, :], XC[:, j % 2, kk].rearrange("p b t -> p (b t)"),
                               kk == 0, kk == 3) for kk in range(4)], waits, sem("bcp"))
            k["bcb", j] = (n, p)

        def dt_bias(j):
            if not ok(j):
                return
            for m, (n, p, tok) in enumerate(k["dtp", j]):
                for a in range(2):
                    k["dtb", j] = put(AC, lambda m=m, a=a, p=p: S.activation(
                        TA[:, 2 * m + a].rearrange("p b t -> p (b t)"), p[:, 160 * a:160 * a + 160],
                        ACT.Identity, bias=PV[:, 1, 2 * m + a:2 * m + a + 1]), (tok,), sem("dtb"))
                bank_free[n].append(k["dtb", j])

        def bc_out(j):
            if not ok(j):
                return
            n, p = k["bcb", j]
            pv = p[:, 0:160].rearrange("p (b c t) -> p c b t", b=8, c=2)
            b = put(AC, lambda: S.activation(BS[:], pv[0:16], ACT.Copy),
                    (k["bc", j], k.get(("bd", j - 1))), sem("bcs"))
            q0 = (2 * j) % 4
            put(AC, lambda: S.activation(CS[32:48, q0:q0 + 2, :, 1:10], pv[32:48, :, :, 0:9], ACT.Copy),
                (k.get(("cd", j - 2)), pre), sem("bcs"))
            put(AC, lambda: S.activation(CS[32:48, q0 + 1, :, 0:1], pv[32:48, 0, :, 9:10], ACT.Copy),
                (), sem("bcs"))
            c = put(AC, lambda: S.activation(CS[32:48, (q0 + 2) % 4, :, 0:1], pv[32:48, 1, :, 9:10], ACT.Copy),
                    (k.get(("cd", j - 1)),), sem("bcs"))
            bank_free[n].append(c)
            for gg in range(2):
                k["bd", j] = put(SP, lambda gg=gg: Y.dma_start(
                    Bd[2 * j:2 * j + 2, gg].rearrange("c n e -> n c e"),
                    BS[:, :, 4 * gg:4 * gg + 4, :].rearrange("n c b t -> n c (b t)")), (b,), sem(f"bd{j % 2}"), dma=True)
                k["cd", j] = put(SP, lambda gg=gg: Y.dma_start(
                    Cd[2 * j:2 * j + 2, gg].rearrange("c n e -> n c e"),
                    CS[32:48, q0:q0 + 2, 4 * gg:4 * gg + 4, :].rearrange("n c b t -> n c (b t)")),
                    (c,), sem(f"cd{j % 2}"), dma=True)

        def softplus_log(j):
            if not ok(j):
                return
            t = put(AC, lambda: S.activation(TB[:], TA[:], ACT.Abs),
                    (k["dtb", j], k["xc", j]), sem("sp"))
            t = put(AC, lambda: S.activation(TB[:], TB[:], ACT.Exp, scale=-1.0), (t,), sem("sp"))
            k["ln", j] = put(AC, lambda: S.activation(TB[:], TB[:], ACT.Ln, bias=ONE[:, 0:1]), (t,), sem("sp"))

        def softplus(j):
            if ok(j):
                k["spl", j] = put(DV, lambda: V.scalar_tensor_tensor(
                    TA[:].rearrange("p a b t -> p (a b t)"), TA[:].rearrange("p a b t -> p (a b t)"), 0.0,
                    TB[:].rearrange("p a b t -> p (a b t)"), ALU.max, ALU.add), (k["ln", j],), sem("spl"))

        def dt_tanh(j):
            if ok(j):
                k["dth", j] = put(AC, lambda: S.activation(TA[:], TA[:], ACT.Tanh, bias=CST[:, 2:3], scale=KD),
                                  (k["spl", j],), sem("dth"))

        def dt_out(j):
            if ok(j):
                k["dt", j] = put(DV, lambda: V.tensor_scalar(DT[:, j % 2], TA[:], 0.0495 / 0.5, 0.0505, ALU.mult, ALU.add),
                                 (k["dth", j], k.get(("z64", j - 2)), k.get(("u", 2 * j - 3))), sem("dt"))

        def dt_x(c):
            j, cc = c // 2, c % 2
            t = slice(10 * cc, 10 * cc + 10)
            k["u", c] = put(DV, lambda: V.tensor_tensor(U(c), DT[:, j % 2, :, :, t], XC[:, j % 2, :, :, t], ALU.mult),
                            (k["dt", j], k["xc", j], k.get(("m1", 2 * (c - 2) + 1))), sem("u"))
            if c == 0:
                k["u", c] = put(DV, lambda: V.memset(U(0).rearrange("p a b t -> p (a b) t")[:, :, 0:9], 0.0),
                                (k["u", c],), sem("u"))

        def gate_tanh(j):
            if ok(j):
                for m, (n, p, tok) in enumerate(k["gate_b", j]):
                    k["tg", j] = put(AC, lambda m=m, p=p: S.activation(
                        TB[:, 2 * m:2 * m + 2].rearrange("p a b t -> p (a b t)"), p[:, 0:320], ACT.Tanh, scale=0.5),
                        (tok, k.get(("spl", j))), sem("tg"))

        def gate(j):
            if not ok(j):
                return
            if j > 0:
                k["sgh", j] = put(PO, lambda: G.tensor_copy(SG[:, j % 2, :, :, 0:1], SG[:, 1 - j % 2, :, :, 20:21]),
                                  (k["sg", j - 1], k.get(("z", 4 * j - 5))), sem("sgh"))
            for m, (n, p, tok) in enumerate(k["gate_b", j]):
                for a in range(2):
                    k["sg", j] = put(DV, lambda m=m, a=a, p=p: V.scalar_tensor_tensor(
                        SG[:, j % 2, 2 * m + a, :, 1:21], TB[:, 2 * m + a], 1.0,
                        p[:, 160 * a:160 * a + 160].rearrange("p (b t) -> p b t", b=8), ALU.add, ALU.mult),
                        (k["tg", j], k.get(("z", 4 * j - 5)), k.get(("dx", j - 2))), sem("sg"))
                bank_free[n].append(k["sg", j])

        def gate_d(j):
            if not ok(j):
                return
            if j > 0:
                put(PO, lambda: G.tensor_copy(DX[:, j % 2, :, :, 0:1], DX[:, 1 - j % 2, :, :, 20:21]),
                    (k["dx", j - 1], k.get(("z", 4 * j - 5))), sem("dx"))
            dv = PV[:, 2, :].unsqueeze(2).unsqueeze(3).to_broadcast([128, 4, 8, 20])
            k["xd", j] = put(PO, lambda: G.tensor_tensor(TC[:], XC[:, j % 2], dv, ALU.mult),
                             (k["xc", j], k.get(("conv", j + 1))), sem("xd"))
            k["dx", j] = put(PO, lambda: G.tensor_tensor(DX[:, j % 2, :, :, 1:21], TC[:], SG[:, j % 2, :, :, 1:21],
                                                         ALU.mult), (k["xd", j], k["sg", j]), sem("dx"))

        def decay_tanh(j, n0, n1):
            if not ok(j):
                return
            for n in range(n0, min(n1, 64)):
                a, s = n // 16, n % 16
                c0 = (2 * j) % 4
                k["z64", j] = put(AC, lambda a=a, s=s: S.activation(
                    DA[:, c0:c0 + 2, :, a, s, 1:11].rearrange("p c b t -> p b c t"),
                    DT[:, j % 2, a].rearrange("p b (c t) -> p b c t", c=2), ACT.Tanh, scale=AS[:, a, s:s + 1]),
                    (k["dt", j], k.get(("scan", 4 * (j - 2) + 3)), pre), sem("z64"))

        def decay_exp(j, r):
            if ok(j):
                c, g = r // 2, r % 2
                v = DA[:, (2 * j + c) % 4, 4 * g:4 * g + 4].rearrange("p b a n t -> p (b a n) t")[:, :, 1:11]
                k["da", 4 * j + r] = put(AC, lambda: S.activation(v, v, ACT.Exp, scale=16.0),
                                         (k["z64", j],), sem("da"))

        def bring(q):
            if 0 <= q < 2 * NC:
                c, g = q // 2, q % 2
                j = c // 2
                k["bb", q] = put(SP, lambda: Y.dma_start(
                    BB[:, q % 3].rearrange("p n b t -> p (n b t)"),
                    Bd[c, g].rearrange("n e -> (n e)").partition_broadcast(128)),
                    (k["bd", j], k.get(("m1", q - 3))), sem(f"bb{q % 3}"), dma=True)
                k["cb", q] = put(SP, lambda: Y.dma_start(
                    CB[:, q % 3].rearrange("p n b t -> p (n b t)"),
                    Cd[c, g].rearrange("n e -> (n e)").partition_broadcast(128)),
                    (k["cd", j], k.get(("hc", q - 3))), sem(f"cb{q % 3}"), dma=True)

        def factor(q):
            g = q % 2
            s = sem("fac")
            sq, y, n, w = FW[:, g, 0], FW[:, g, 1], FW[:, g, 2], FW[:, g, 3]
            t = put(DV, lambda: V.tensor_scalar(sq, NP(g), 1e-30, None, ALU.max),
                    (k["nrm", q - 2], k.get(("ca", q - 2))), s)
            k["nread", q - 2] = t
            yield
            t = put(DV, lambda: V.tensor_scalar(FI[:, g], sq.bitcast(I32), 1, None, ALU.logical_shift_right),
                    (t,), s)
            yield
            t = put(DV, lambda: V.tensor_scalar(y.bitcast(I32), FI[:, g], -1, 0x5f3759df, ALU.mult, ALU.add),
                    (t,), s)
            yield
            t = put(DV, lambda: V.tensor_tensor(n, sq, y, ALU.mult), (t,), s)
            yield
            t = put(DV, lambda: V.tensor_tensor(w, n, y, ALU.mult), (t,), s)
            yield
            t = put(DV, lambda: V.scalar_tensor_tensor(w, w, -10.0 / 3, w, ALU.add, ALU.mult), (t,), s)
            yield
            t = put(DV, lambda: V.scalar_tensor_tensor(y, w, 5.0, y, ALU.add, ALU.mult), (t,), s)
            yield
            t = put(DV, lambda: V.tensor_tensor(n, sq, y, ALU.mult), (t,), s)
            yield
            t = put(DV, lambda: V.tensor_tensor(w, n, y, ALU.mult), (t,), s)
            yield
            t = put(DV, lambda: V.scalar_tensor_tensor(n, w, -64.0 / 3, n, ALU.add, ALU.mult), (t,), s)
            yield
            t = put(DV, lambda: V.tensor_scalar(n, n, -27.0 / 1024 / 20, 1e-8 / 20, ALU.mult, ALU.add), (t,), s)
            yield
            k["fac", q] = put(DV, lambda: V.reciprocal(FC[:, g], n), (t,), s)

        def mult(q, u):
            c, g = q // 2, q % 2
            j, cc, b = c // 2, c % 2, 4 * g + u
            o = DBX(u).rearrange("p (a n t) -> p a n t", a=4, n=16)[:, :, :, 1:11]
            i0 = U(c)[:, :, b, :].unsqueeze(2).to_broadcast([128, 4, 16, 10])
            i1 = BB[:, q % 3, :, u, :].unsqueeze(1).to_broadcast([128, 4, 16, 10])
            k["m1", q] = k["m1", q, u] = put(DV, lambda: V.tensor_tensor(o, i0, i1, ALU.mult), (k["bb", q], k["u", c], k.get(("dbx", u % 2))), sem("m1"))

        def carry(q, u):
            o = PM[:, 640:640 + 2 * CH].rearrange("p (u a t) -> p u a t", u=2, t=11)[:, :, :, 0]
            w = [k.get(("dbx", 0)), k.get(("dbx", 1))]
            if q < 2:
                t = put(DV, lambda: V.memset(o, 0.0), w, sem("ca"))
            else:
                i = H[:, (q - 2) % 3, u:u + 2].rearrange("p u (a t) -> p u a t", t=11)[:, :, :, 10]
                f = FC[:, q % 2, u:u + 2].unsqueeze(2).to_broadcast([128, 2, 64])
                t = put(DV, lambda: V.scalar_tensor_tensor(o, f, 1.0, i, ALU.min, ALU.mult), w + [k["fac", q]], sem("ca"))
            k["ca", q] = k["ca", q, u] = k["ca", q, u + 1] = t

        def scan(q, u):
            c, g = q // 2, q % 2
            a0 = DA[:, c % 4, 4 * g + u].rearrange("p a n t -> p (a n t)")
            k["scan", q] = put(DV, lambda: V.tensor_tensor_scan(
                H[:, q % 3, u], a0, DBX(u), 0.0, ALU.mult, ALU.add),
                (k["m1", q, u], k["ca", q, u], k["da", q], k.get(("ys", q - 3)), ze if q < 3 else None), sem("scan"))
            k["scan", q, u] = k["dbx", u % 2] = k["scan", q]

        def squared(q, u):
            g = q % 2
            h = H[:, q % 3, u].rearrange("p (a t) -> p a t", t=11)[:, :, 10]
            k["sqs", q] = put(DV, lambda: V.tensor_tensor_reduce(
                out=JK[:, u % 2], in0=h, in1=h, scale=1.0, scalar=0.0, op0=ALU.mult, op1=ALU.add,
                accum_out=SS[:, g, u:u + 1]), (k["scan", q, u], k.get(("nrm", q - 2)), k.get(("jk", u % 2))), sem("sqs"))
            k["jk", u % 2] = k["sqs", q]

        def hc(q, u):
            h = H[:, q % 3, u].rearrange("p (a n t) -> p a n t", a=4, n=16)[:, :, :, 0:10]
            i1 = CB[:, q % 3, :, u, :].unsqueeze(1).to_broadcast([128, 4, 16, 10])
            k["hc", q] = put(PO, lambda: G.tensor_tensor(h, h, i1, ALU.mult),
                             (k["scan", q, u], k["cb", q]), sem("hc"))

        def norm_sum(q):
            k["nrm", q] = mms([(NP(q % 2), ONE[:], SS[:, q % 2], True, True)],
                              (k["sqs", q], k.get(("nread", q - 2)), k.get(("z", q - 2))), sem("nrm"))

        def y_sum(q, n0, n1):
            if not 0 <= q < 2 * NC:
                return
            hv = H[:, q % 3].rearrange("p u (a n t) -> p u a n t", a=4, n=16)
            k["ys", q] = mms([(YP(q).rearrange("p (u a t) -> p u a t", u=4, a=4), ID[:], hv[:, :, :, n, 0:10],
                               n == 0, n == 15) for n in range(n0, n1)],
                             (k["hc", q], k.get(("z", q - 2)), k.get(("nread", q))), sem("ys"))

        def z_out(q):
            if not 0 <= q < 2 * NC:
                return
            c, g = q // 2, q % 2
            j, cc = c // 2, c % 2

            def vw(t):
                return t.rearrange("p a b t -> p b a t")
            o = vw(Z[:, :, 4 * g:4 * g + 4, 10 * cc:10 * cc + 10])
            yv = YP(q).rearrange("p (u a t) -> p u a t", u=4, a=4)
            t = put(DV, lambda: V.tensor_tensor(
                o, yv, vw(SG[:, j % 2, :, 4 * g:4 * g + 4, 10 * cc:10 * cc + 10]), ALU.mult),
                (k["ys", q], k.get(("op", j - 1)), k["sg", j], k.get(("sgh", j))), sem("zm"))
            k["z", q] = put(DV, lambda: V.tensor_tensor(
                o, o, vw(DX[:, j % 2, :, 4 * g:4 * g + 4, 10 * cc:10 * cc + 10]), ALU.add),
                (t, k["dx", j]), sem("z"))

        def load_res(i):
            if ok(i):
                for g in range(2):
                    for b in range(4):
                        k["xr", i] = put(SP, lambda g=g, b=b: Y.dma_start(
                            XR[20 * b:20 * b + 20, g, :], d["xp"][4 * g + b, T * i:T * i + T, :]),
                            (k.get(("v", i - 1)),), sem("xr"), dma=True)

        def out_proj(i):
            if ok(i):
                n, p, waits = bank()
                zf = Z[:].rearrange("p a b t -> p a (b t)")
                k["op", i] = mms([(p[0:80, 256 * g:256 * g + 256], zf[:, a, 80 * g:80 * g + 80], WO[:, a, :],
                                   a == 0, a == 3) for g in range(2) for a in range(4)],
                                 [k["z", 4 * i + 3], pre] + waits, sem("op"))
                k["opb", i] = (n, p)

        def residual(i):
            if ok(i):
                n, p = k["opb", i]
                k["v", i] = put(DV, lambda: V.scalar_tensor_tensor(
                    VV[:].rearrange("p a b -> p (a b)"), XR[:].rearrange("p a b -> p (a b)"), 2.0, p[0:80, :],
                    ALU.mult, ALU.add), (k["op", i], k["xr", i], k.get(("x2d", i - 1)), k.get(("tr", i - 1))),
                    sem("v"))
                bank_free[n].append(k["v", i])
                for g in range(2):
                    t = put(DV, lambda g=g: V.bn_stats(BN[:, g], VV[:, g]), (k["v", i],), sem("bn"))
                for g in range(2):
                    k["mv", i] = put(DV, lambda g=g: V.bn_aggr(MVR[:, g], BN[:, g]), (t,), sem("mv"))

        def ln_root(i):
            if ok(i):
                k["sd", i] = put(AC, lambda: S.activation(SD[:], MVR[:, :, 1], ACT.Ln, bias=CST[0:80, 1:2]),
                                 (k["mv", i], k.get(("x2", i - 1))), sem("sd"))

        def ln_inv(i):
            if ok(i):
                k["isd", i] = put(AC, lambda: S.activation(SD[:], SD[:], ACT.Exp, scale=-0.5), (k["sd", i],), sem("isd"))

        def ln_out(i):
            if ok(i):
                for g in range(2):
                    k["x2", i] = put(DV, lambda g=g: V.tensor_scalar(
                        VV[:, g], VV[:, g], MVR[:, g, 0:1], SD[:, g:g + 1], ALU.subtract, ALU.mult),
                        (k["isd", i],), sem("x2"))
                for g in range(2):
                    for b in range(4):
                        k["x2d", i] = put(SP, lambda g=g, b=b: Y.dma_start(
                            X2d[4 * g + b, T * i:T * i + T, :], VV[20 * b:20 * b + 20, g, :]),
                            (k["x2", i],), sem("x2d"), dma=True)

        def transposed(i):
            if ok(i):
                n, p, waits = bank()
                tok = None
                for g in range(2):
                    for a in range(2):
                        o = p[:, 80 * (2 * g + a):80 * (2 * g + a) + 80]
                        tok = put(PE, lambda o=o, g=g, a=a: M.transpose(
                            o, VV[:, g, 128 * a:128 * a + 128], ID[0:80, 0:80]),
                            [k["x2", i]] + waits if (g, a) == (0, 0) else (), sem("tr"))
                k["tr", i] = tok
                k["x2t", i] = put(AC, lambda: S.activation(X2T[:].rearrange("p a b -> p (a b)"), p[:, 0:320],
                                                           ACT.Copy), (tok, k.get(("lg", i - 1))), sem("x2t"))
                bank_free[n].append(k["x2t", i])

        def logits(i):
            if ok(i):
                n, p, waits = bank()
                k["lg", i] = mms([(p[0:80, 8 * g:8 * g + 8], X2T[:, 2 * g + a, :], WR[:, a, :], a == 0, a == 1)
                                  for g in range(2) for a in range(2)], [k["x2t", i]] + waits, sem("lg"))
                k["lgb", i] = (n, p)

        def logits_out(i):
            if ok(i):
                n, p = k["lgb", i]
                t = put(DV, lambda: V.tensor_copy(LGS[:].rearrange("p a b -> p (a b)"), p[0:80, 0:16]),
                        (k["lg", i], k.get(("lgd", i - 1))), sem("lgs"))
                bank_free[n].append(t)
                for g in range(2):
                    for b in range(4):
                        k["lgd", i] = put(SP, lambda g=g, b=b: Y.dma_start(
                            LGd[4 * g + b, T * i:T * i + T, :], LGS[20 * b:20 * b + 20, g, :]),
                            (t,), sem("lgd"), dma=True)

        def window(i):
            live = ok(i)
            if i == NB + 1:
                transposed(i - 2)
                logits(i - 2)
                logits_out(i - 2)
                return
            for s in range(16):
                r, u = s // 4, s % 4
                q = 4 * i + r
                if s == 0:
                    load_x(i + 4)
                    project(i + 2, 0, "br")
                    halo(i + 2)
                if s == 1:
                    dt_out(i + 1)
                if s == 2:
                    transposed(i - 2)
                if 2 <= s < 6:
                    conv(i + 2, s - 2)
                if s == 3:
                    project(i + 1, 512, "gate")
                if s == 4:
                    gate_tanh(i + 1)
                if s == 7:
                    gate(i + 1)
                    out_proj(i - 1)
                    logits(i - 2)
                    if live:
                        dt_x(2 * i + 1)
                if s == 8:
                    gate_d(i + 1)
                if s == 9:
                    silu(i + 2)
                    logits_out(i - 2)
                    residual(i - 1)
                    load_res(i)
                    dt_proj(i + 2)
                    squares(i + 3)
                if s == 12:
                    softplus_log(i + 2)
                    roots(i + 3)
                    ln_root(i - 1)
                    bc_out(i + 2)
                    inv_roots(i + 3)
                    ln_inv(i - 1)
                if s == 14:
                    softplus(i + 2)
                    dt_tanh(i + 2)
                if s == 15:
                    normed(i + 3)
                    ln_out(i - 1)
                if 1 <= s < 12:
                    decay_tanh(i + 1, 6 * s - 6, 6 * s)
                elif s > 11:
                    decay_exp(i + 1, s - 12)
                if s == 1:
                    branch_out(i + 2)
                if s == 8:
                    silu_tanh(i + 2)
                if s == 11:
                    dt_bias(i + 2)
                    bc_proj(i + 2)
                    sum_squares(i + 3)
                if u == 0:
                    if live:
                        if r == 0:
                            dt_x(q // 2)
                if u == 0:
                    y_sum(q - 2, 11, 16)
                if u == 3:
                    y_sum(q - 1, 6, 11)
                if live:
                    if u % 2 == 0:
                        mult(q, u)
                        if u == 0:
                            rest(DV)
                        carry(q, u)
                        mult(q, u + 1)
                    scan(q, u)
                    hc(q, u)
                if u == 2:
                    z_out(q - 2)
                    if 0 <= q - 1 < 2 * NC - 2:
                        assert ("nread", q - 1) in k
                    y_sum(q - 1, 0, 6)
                if live:
                    if u > 0:
                        squared(q, u - 1)
                    if u == 1 and 1 <= q < 2 * NC - 1:
                        side = factor(q + 1)
                        next(side)
                        DV.side = side
                    if u == 3:
                        squared(q, 3)
                        norm_sum(q)
                if u == 3 and q + 2 >= 0:
                    bring(q + 2)

        for i in range(-4, NB + 2):
            window(i)
        for name in ("x2d", "lgd", "ya0", "bd0", "cd0", "bd1", "cd1"):
            if name in sems:
                put(SP, None, ((sems[name], sems[name].n),))
        run_block(nc, qs)


def moe_phase(nc, d, YA, X2d, LGd, out):
    ctx = ExitStack()
    with ctx:
        def sb(name, shape, dt=F32):
            return ctx.enter_context(nc.sbuf_tensor(name, shape, dt))

        sems = {}

        def sem(name):
            if name not in sems:
                sems[name] = Sem(ctx.enter_context(nc.semaphore("m_" + name)))
            return sems[name]

        qs = {k: Queue() for k in ("sp", "act", "dve", "pool", "pe")}
        SP, AC, DV, PO, PE = qs["sp"], qs["act"], qs["dve"], qs["pool"], qs["pe"]
        V, S, G, M, Y = nc.vector, nc.scalar, nc.gpsimd, nc.tensor, nc.sync

        W1 = sb("W1", [128, 2, 2, 1024])
        W2 = sb("W2", [128, 2, 8, 256])
        B1 = sb("B1", [128, 8, 8])
        B2 = sb("B2", [128, 8, 256])
        XR = sb("XRE", [128, 2, 6, 256])
        XT = sb("XTE", [128, 2, 768])
        HT = sb("HT", [128, 8, 768])
        YS = sb("YS", [128, 3, 2, 256])
        LO = sb("LO", [128, 2, 2, 16, 128])
        HI = sb("HI", [128, 2, 64, 96])
        GT = sb("GT", [128, 2, 48])
        IOL = sb("IOL", [128, 128])
        TK = sb("TK", [128, 64])
        ID = sb("ID2", [128, 128])
        ONE = sb("ONE2", [128, 128])
        TRI = sb("TRI", [128, 128])
        IO = sb("IO", [128, 8])
        LG = sb("LG", [128, 64, 8])
        P = sb("P", [128, 64, 8])
        VL = sb("VL", [128, 64, 8])
        OH = sb("OH", [128, 2, 64, 8])
        MM = sb("MM", [128, 64, 8])
        CN = sb("CN", [128, 8, 64])
        MK = sb("MK", [128, 8, 64])
        CI = sb("CI", [128, 8, 64])
        PO_ = sb("POS", [128, 64, 8])
        R = sb("R", [128, 16, 64])
        IX = sb("IX", [128, 3, 64], I32)
        IG = sb("IG", [128, 2, 48], I32)
        BN = sb("BN2", [128, 4, 8, 6])
        MV = sb("MV2", [128, 4, 8, 2])
        SD = sb("SD2", [128, 4, 8])
        NM = sb("NM", [128, 4, 8])
        EP = sb("EP", [128, 1])
        PB = [ctx.enter_context(nc.psum_tensor(f"PE{i}", [128, 512], F32)) for i in range(8)]

        k = {}
        lg = put(SP, lambda: Y.dma_start(ID[:], d["ident"]), (), sem("ld"), dma=True)
        lg = put(SP, lambda: Y.dma_start(TRI[:], d["tri"]), (), sem("ld"), dma=True)
        lg = put(SP, lambda: Y.dma_start(IO[:], d["iota"].to_broadcast([128, 8])), (), sem("ld"), dma=True)
        for b in range(8):
            lg = put(SP, lambda b=b: Y.dma_start(
                LG[:, 8 * b:8 * b + 8, :], LGd[b, 10:10 + L, :].rearrange("(j p) e -> p j e", p=128)),
                (), sem("ld"), dma=True)
        lg = put(SP, lambda: Y.dma_start(IOL[:], d["lanes"].to_broadcast([128, 128])), (), sem("ld"), dma=True)
        lg = put(SP, lambda: Y.dma_start(TK[:], d["rows"]), (), sem("ld"), dma=True)
        put(AC, lambda: S.dma_start(B1[:], d["b1"]), (), sem("bl"), dma=True)
        bl = put(AC, lambda: S.dma_start(B2[:].rearrange("p e n -> p (e n)"),
                                         d["b2"].rearrange("e n -> (e n)").partition_broadcast(128)),
                 (), sem("bl"), dma=True)

        s = sem("rt")

        def dv(fn, *waits):
            k["c"] = put(DV, fn, (k.get("c"),) + waits, s)
            return k["c"]

        def bc(t):
            return t.unsqueeze(2).to_broadcast([128, 64, 8])

        dv(lambda: V.memset(ONE[:], 1.0))
        dv(lambda: V.memset(EP[:], 1e-5))
        dv(lambda: V.memset(MK[:], 1.0))
        dv(lambda: V.memset(MK[:, :, 0:1], 0.0))
        dv(lambda: V.tensor_reduce(R[:, 0], LG[:], AX.X, ALU.max), lg)
        t = dv(lambda: V.tensor_tensor(P[:], LG[:], bc(R[:, 0]), ALU.subtract))
        a = put(AC, lambda: S.activation(P[:], P[:], ACT.Exp), (t,), sem("ra"))
        dv(lambda: V.tensor_reduce(R[:, 1], P[:], AX.X, ALU.add), a)
        dv(lambda: V.reciprocal(R[:, 1], R[:, 1]))
        dv(lambda: V.tensor_tensor(P[:], P[:], bc(R[:, 1]), ALU.mult))
        for n in range(2):
            pk, ek = R[:, 2 + n], R[:, 4 + n]
            iob = IO[:].unsqueeze(1).to_broadcast([128, 64, 8])
            dv(lambda pk=pk: V.tensor_reduce(pk, P[:], AX.X, ALU.max))
            dv(lambda pk=pk: V.tensor_tensor(VL[:], P[:], bc(pk), ALU.is_ge))
            dv(lambda: V.scalar_tensor_tensor(VL[:], VL[:], -100.0, iob, ALU.mult, ALU.add))
            dv(lambda ek=ek: V.tensor_reduce(ek, VL[:], AX.X, ALU.min))
            dv(lambda ek=ek, n=n: V.tensor_tensor(OH[:, n], VL[:], bc(ek), ALU.is_equal))
            if n == 0:
                dv(lambda: V.scalar_tensor_tensor(P[:], OH[:, 0], -4.0, P[:], ALU.mult, ALU.add))
        t = dv(lambda: V.tensor_tensor(MM[:], OH[:, 0], OH[:, 1], ALU.add))
        put(PE, lambda: M.matmul(PB[0][:], TRI[:], MM[:].rearrange("p j e -> p (j e)"), start=True, stop=True),
            (t, lg), sem("rp"))
        t = put(PE, lambda: M.matmul(PB[1][:], ONE[:], MM[:].rearrange("p j e -> p (j e)"), start=True, stop=True),
                (), sem("rp"))
        k["cn"] = dv(lambda: V.tensor_copy(CN[:], PB[1][:].rearrange("p (j e) -> p e j", e=8)), t)
        dv(lambda: V.tensor_tensor_scan(CI[:].rearrange("p e j -> p (e j)"), MK[:].rearrange("p e j -> p (e j)"),
                                        CN[:].rearrange("p e j -> p (e j)"), 0.0, ALU.mult, ALU.add))
        dv(lambda: V.tensor_tensor(CI[:], CI[:], CN[:], ALU.subtract))
        dv(lambda: V.tensor_tensor(PO_[:], PB[0][:].rearrange("p (j e) -> p j e", e=8),
                                   CI[:].rearrange("p e j -> p j e"), ALU.add))
        dv(lambda: V.tensor_tensor(R[:, 6], R[:, 2], R[:, 3], ALU.add))
        dv(lambda: V.reciprocal(R[:, 6], R[:, 6]))
        for n in range(2):
            dv(lambda n=n: V.tensor_tensor(VL[:], PO_[:], OH[:, n], ALU.mult))
            dv(lambda: V.tensor_reduce(R[:, 7], VL[:], AX.X, ALU.add))
            dv(lambda: V.tensor_scalar(R[:, 1], R[:, 7], float(CAP), 1000.0, ALU.is_ge, ALU.mult))
            dv(lambda: V.tensor_copy(IX[:, 0], R[:, 7]))
            dv(lambda: V.tensor_scalar(IX[:, 1], IX[:, 0], 7, None, ALU.logical_shift_right))
            dv(lambda: V.tensor_scalar(IX[:, 2], IX[:, 0], 127, None, ALU.bitwise_and))
            dv(lambda: V.tensor_copy(R[:, 10], IX[:, 1]))
            dv(lambda n=n: V.tensor_copy(R[:, 14 + n], IX[:, 2]))
            dv(lambda n=n: V.tensor_scalar(R[:, 11], R[:, 4 + n], 100.0, 6.0, ALU.add, ALU.mult))
            dv(lambda: V.tensor_tensor(R[:, 10], R[:, 10], R[:, 11], ALU.add))
            dv(lambda n=n: V.tensor_tensor(R[:, 8 + n], R[:, 10], R[:, 1], ALU.add))
            k["g"] = dv(lambda n=n: V.tensor_tensor(R[:, 12 + n], R[:, 2 + n], R[:, 6], ALU.mult))
        io48 = IOL[:, 0:48].unsqueeze(1).to_broadcast([128, 16, 48])

        def cols(t, j):
            return t[:, j].unsqueeze(2).to_broadcast([128, 16, 48])

        def columns(c, n):
            j = slice(16 * c, 16 * c + 16)
            h, g = HI[:, n, j, 0:48], HI[:, n, j, 48:96]
            eng, q = (G, PO) if n else (V, DV)
            t = put(DV, lambda: V.tensor_tensor(g, cols(R[:, 8 + n], j), io48, ALU.is_equal),
                    (k["g"],), sem("eq"))
            put(q, lambda: eng.tensor_tensor(h, g, cols(TK, j), ALU.mult), (t,), sem(f"hi{n}"))
            k["hi", c, n] = put(q, lambda: eng.tensor_tensor(g, g, cols(R[:, 12 + n], j), ALU.mult),
                                ((sem(f"hi{n}"), sem(f"hi{n}").n),), sem(f"hi{n}"))

        def lanes(c, n):
            k["lo", c, n] = put(DV, lambda: V.tensor_tensor(
                LO[:, c % 2, n], R[:, 14 + n, 16 * c:16 * c + 16].unsqueeze(2).to_broadcast([128, 16, 128]),
                IOL[:].unsqueeze(1).to_broadcast([128, 16, 128]), ALU.is_equal),
                (k["g"], k.get(("gi", c - 2, n))), sem("lo"))

        GP = PB[1][:, 0:96]
        for c in range(4):
            columns(c, 1)
            columns(c, 0)
            for n in range(2):
                lanes(c, n)
                for j in range(16):
                    t = put(PE, lambda c=c, n=n, j=j: M.matmul(
                        GP, LO[:, c % 2, n, j], HI[:, n, 16 * c + j], start=(c, n, j) == (0, 0, 0),
                        stop=(c, n, j) == (3, 1, 15)), (k["lo", c, n], k["hi", c, n], k["cn"]), sem("gi"))
                k["gi", c, n] = t
        dv(lambda: V.tensor_copy(GT[:], GP.rearrange("p (a b) -> p a b", a=2)), t)
        dv(lambda: V.tensor_copy(IG[:, 0], GT[:, 0]))
        dv(lambda: V.tensor_scalar(GT[:, 0], GT[:, 0], 0.5, 1e6, ALU.is_lt, ALU.mult))
        dv(lambda: V.tensor_copy(IG[:, 1], GT[:, 0]))
        k["ix"] = dv(lambda: V.tensor_tensor(IG[:, 1], IG[:, 1], IG[:, 0], ALU.add))

        def load_w(e):
            if e < E:
                put(AC, lambda: S.dma_start(W1[:, e % 2], d["w1"][e].rearrange("(a p) n -> p a n", p=128)),
                    (k.get(("h", e - 2)),), sem(f"wl{e % 2}"), dma=True)
                k["w", e] = put(AC, lambda: S.dma_start(W2[:, e % 2], d["w2"][e].rearrange("(a p) n -> p a n", p=128)),
                                (k.get(("y", e - 2)),), sem(f"wl{e % 2}"), dma=True)

        XRW = X2d.rearrange("b r n -> (b r) n")

        def load_e(e):
            if e < E:
                for c in range(6):
                    k["xe", e, c // 2] = put(PO, lambda c=c: G.indirect_dma_start(
                        out=XR[:, e % 2, c], out_offset=None, in_=XRW,
                        in_offset=bass.IndirectOffsetOnAxis(ap=IG[:, 0, 6 * e + c:6 * e + c + 1].bitcast(U32), axis=0),
                        bounds_check=B * LP - 1, oob_is_err=False), (k["ix"], k.get(("xt", e - 2))),
                        sem(f"xe{e % 2}{c // 2}"), dma=True)

        free = {}
        nb = [2]

        def bank():
            n = nb[0] % 8
            nb[0] += 1
            return n, PB[n], [free.get(n)]

        load_w(0)
        load_w(1)
        load_e(0)
        load_e(1)
        for e in range(E):
            for c in range(3):
                n, p, waits = bank()
                for a in range(2):
                    for h in range(2):
                        o = p[:, 256 * a + 128 * h:256 * a + 128 * h + 128]
                        t = put(PE, lambda o=o, a=a, h=h, c=c, e=e: M.transpose(
                            o, XR[:, e % 2, 2 * c + h, 128 * a:128 * a + 128], ID[:]),
                            waits + [k["xe", e, c], lg, k["ix"]], sem("xt"))
                free[n] = put(DV, lambda p=p, c=c: V.tensor_copy(
                    XT[:, :, 256 * c:256 * c + 256], p[:].rearrange("p (a n) -> p a n", a=2)),
                    (t, k.get(("h", e - 1))), sem("xtc"))
            k["xt", e] = t
            xc = free[n]
            load_e(e + 2)
            for m in range(8):
                for h in range(2):
                    n, p, waits = bank()
                    for a in range(2):
                        t = put(PE, lambda p=p, a=a, m=m, h=h, e=e: M.matmul(
                            p[:, 0:384], W1[:, e % 2, a, 128 * m:128 * m + 128], XT[:, a, 384 * h:384 * h + 384],
                            start=a == 0, stop=a == 1), waits + [xc, k["w", e]], sem("h"))
                    if h == 0:
                        free[n] = r0 = put(AC, lambda p=p, m=m, h=h, e=e: S.activation(
                            HT[:, m, 384 * h:384 * h + 384], p[:, 0:384], ACT.Relu, bias=B1[:, e, m:m + 1]),
                            (t, bl, k.get(("y", e - 1))), sem("ra"))
                    else:
                        free[n] = r1 = put(DV, lambda p=p, m=m, h=h, e=e: V.tensor_scalar(
                            HT[:, m, 384 * h:384 * h + 384], p[:, 0:384], B1[:, e, m:m + 1], 0.0,
                            ALU.add, ALU.max), (t, bl, k.get(("y", e - 1))), sem("rv"))
            k["h", e] = t
            before = [k["yo", i] for i in range(3 * e - 3, 3 * e) if i >= 0]
            for c in range(3):
                n, p, waits = bank()
                for h in range(2):
                    for m in range(8):
                        t = put(PE, lambda p=p, m=m, h=h, c=c, e=e: M.matmul(
                            p[:, 256 * h:256 * h + 256], HT[:, m, 128 * (2 * c + h):128 * (2 * c + h) + 128],
                            W2[:, e % 2, m, :], start=m == 0, stop=m == 7), waits + [r0, r1], sem("y"))
                i = 3 * e + c
                free[n] = t2 = put(DV, lambda p=p, i=i, e=e: V.tensor_tensor(
                    YS[:, i % 3], p[:].rearrange("p (h n) -> p h n", h=2),
                    B2[:, e].unsqueeze(1).to_broadcast([128, 2, 256]), ALU.add),
                    (t, k.get(("yo", i - 3)), bl), sem("ys"))
                for h in range(2):
                    t3 = put(AC, lambda i=i, h=h: S.activation(
                        YS[:, i % 3, h], YS[:, i % 3, h], ACT.Copy, scale=GT[:, 1, 2 * i + h:2 * i + h + 1]),
                        (t2,), sem("yg"))
                    k["yo", i] = put(PO, lambda i=i, h=h: G.indirect_dma_start(
                        out=YA, out_offset=bass.IndirectOffsetOnAxis(
                            ap=IG[:, 1, 2 * i + h:2 * i + h + 1].bitcast(U32), axis=0),
                        in_=YS[:, i % 3, h], in_offset=None, bounds_check=B * LP - 1, oob_is_err=False,
                        compute_op=ALU.add), [t3] + before, sem(f"yo{i % 3}"), dma=True)
            k["y", e] = t
            load_w(e + 2)

        XF = HI[:].rearrange("p a b c -> p (a b c)").rearrange("p (k j n) -> p k j n", k=6, j=8)
        YF = HT[:].rearrange("p a b -> p (a b)").rearrange("p (k j n) -> p k j n", k=3, j=8)
        YB = YA.rearrange("(b r) n -> b r n", b=B)

        def fetch_x(b):
            k["xf", b] = put(SP, lambda: Y.dma_start(
                XF[:, b % 6], X2d[b, 10:10 + L, :].rearrange("(j p) n -> p j n", p=128)),
                (k["ix"], k.get(("out", b - 6))), sem(f"xf{b % 2}"), dma=True)

        def fetch_y(b):
            k["yf", b] = put(SP, lambda: Y.dma_start(
                YF[:, b % 3], YB[b, 10:10 + L, :].rearrange("(j p) n -> p j n", p=128)),
                (k["yo", 21], k["yo", 22], k["yo", 23], k["y", E - 1], k.get(("sum", b - 3))), sem(f"yf{b % 3}"), dma=True)

        def added(b):
            eng, q = (G, PO) if b % 2 else (V, DV)
            x = XF[:, b % 6]
            k["sum", b] = put(q, lambda: eng.tensor_tensor(x, x, YF[:, b % 3], ALU.add),
                              (k["xf", b], k["yf", b]), sem(f"sum{b % 2}"))

        def norm(b):
            x = XF[:, b % 6]
            t = k["sum", b]
            for j in range(8):
                t1 = put(DV, lambda j=j: V.bn_stats(BN[:, b % 4, j], x[:, j]),
                         (t, k.get(("x3", b - 4))), sem("bn"))
            for j in range(8):
                t2 = put(DV, lambda j=j: V.bn_aggr(MV[:, b % 4, j], BN[:, b % 4, j]), (t1,), sem("mv"))
            k["sd", b] = put(AC, lambda: S.activation(SD[:, b % 4], MV[:, b % 4, :, 1], ACT.Sqrt, bias=EP[:]),
                             (t2, k.get(("x3", b - 4))), sem("sd"))

        def finish(b):
            x = XF[:, b % 6]
            t = put(DV, lambda: V.reciprocal(SD[:, b % 4], SD[:, b % 4]), (k["sd", b],), sem("rc"))
            t = put(DV, lambda: V.scalar_tensor_tensor(NM[:, b % 4], MV[:, b % 4, :, 0], -1.0, SD[:, b % 4],
                                                       ALU.mult, ALU.mult), (t, k.get(("x3", b - 4))), sem("rc"))
            for j in range(8):
                k["x3", b] = t2 = put(AC, lambda j=j: S.activation(
                    x[:, j], x[:, j], ACT.Identity, bias=NM[:, b % 4, j:j + 1], scale=SD[:, b % 4, j:j + 1]),
                    (t,), sem("x3"))
                if j % 4 == 3:
                    r0 = L * b + 128 * (j - 3)
                    k["out", b] = put(SP, lambda j=j, r0=r0: Y.dma_start(
                        out[r0:r0 + 512, :].rearrange("(j p) n -> p j n", p=128), x[:, j - 3:j + 1]),
                        (t2,), sem(f"out{b % 6}"), dma=True)

        for b in range(6):
            fetch_x(b)
        for b in range(3):
            fetch_y(b)
        added(0)
        added(1)
        for b in range(B + 1):
            if b < B:
                norm(b)
            if b + 3 < B:
                fetch_y(b + 3)
            if b + 2 < B:
                added(b + 2)
            if b > 0:
                finish(b - 1)
                if b + 5 < B:
                    fetch_x(b + 5)
        for b in range(B - 6, B):
            put(SP, None, (k["out", b],))
        run_block(nc, qs)


def build(nc, d, out):
    YA = nc.dram_tensor("YA", [B * LP, DM], F32, kind="Internal").ap()
    X2d = nc.dram_tensor("X2d", [B, LP, DM], F32, kind="Internal").ap()
    LGd = nc.dram_tensor("LGd", [B, LP, E], F32, kind="Internal").ap()
    Bd = nc.dram_tensor("Bd", [NC, 2, NS, 40], F32, kind="Internal").ap()
    Cd = nc.dram_tensor("Cd", [NC, 2, NS, 40], F32, kind="Internal").ap()
    ssm_phase(nc, d, YA, X2d, LGd, Bd, Cd)
    moe_phase(nc, d, YA, X2d, LGd, out)


def kernel(**inputs):
    import concourse.bacc as bacc
    from concourse.bass_utils import run_bass_kernel_spmd

    a = {n: np.asarray(v) for n, v in inputs.items()}
    x = a["L0_attn_x"]
    xp = np.zeros((B, LP + 1, DM), np.float32)
    xp[:, 10:10 + L] = x
    xT = xp[:, 1:].reshape(B, NB, T, 2, 128).transpose(1, 4, 3, 0, 2).reshape(NB, 128, 2, B * T)
    wbc = np.zeros((DI, 64), np.float32)
    wbc[:, 0:16] = a["L0_attn_W_B"].T
    wbc[:, 32:48] = a["L0_attn_W_C"].T
    arrays = {
        "xT": xT, "xp": xp[:, :LP],
        "w_in": a["L0_attn_W_in"].T, "w_dt": a["L0_attn_W_dt"].T, "w_bc": wbc, "w_out": a["L0_attn_W_out"].T,
        "a_log": a["L0_attn_A_log"], "conv_w": a["L0_attn_conv_w"].reshape(DI, 4), 
        "vecs": np.stack([a[n].reshape(4, 128).T for n in ("L0_attn_conv_b", "L0_attn_b_dt", "L0_attn_D_param")], 1),
        "norm_w": a["L0_attn_norm_w"].reshape(2, 128).T,
        "res": a["L0_attn_residual_scale"].reshape(1, 1), "w_router": a["L0_ffn_w_router"],
        "w1": a["L0_ffn_w1"], "b1": a["L0_ffn_b1"].reshape(E, 8, 128).transpose(2, 0, 1), "w2": a["L0_ffn_w2"], "b2": a["L0_ffn_b2"],
        "ident": np.eye(128, dtype=np.float32), "tri": np.triu(np.ones((128, 128), np.float32), 1),
        "lanes": np.arange(128, dtype=np.float32).reshape(1, 128),
        "rows": (np.arange(B)[None, :, None] * LP + 10 + np.arange(8)[None, None, :] * 128
                 + np.arange(128)[:, None, None]).reshape(128, 64).astype(np.float32),
        "iota": np.arange(8, dtype=np.float32).reshape(1, 8),
    }
    nc = bacc.Bacc("TRN2", target_bir_lowering=False, num_devices=1)
    feed, d = {}, {}
    for n, v in arrays.items():
        v = np.ascontiguousarray(v)
        feed[f"in_{n}"] = v
        d[n] = nc.dram_tensor(f"in_{n}", v.shape, mybir.dt.from_np(v.dtype), kind="ExternalInput").ap()
    out = nc.dram_tensor("out_y", [B * L, DM], F32, kind="ExternalOutput").ap()
    build(nc, d, out)
    r = run_bass_kernel_spmd(nc, [feed], core_ids=[0])
    return r.results[0]["out_y"].reshape(B, L, DM)
```
